# Optimizing a Trainium2 kernel written in Bass

```python
import numpy as np
import jax
import jax.numpy as jnp

def _softmax(x, axis=-1):
    return jax.nn.softmax(x, axis=axis)

def _gelu(x):
    return jax.nn.gelu(x, approximate=True)

def _silu(x):
    return jax.nn.silu(x)

def _sigmoid(x):
    return jax.nn.sigmoid(x)

def _layernorm(x, axis=-1, eps=1e-05):
    m = jnp.mean(x, axis=axis, keepdims=True)
    v = jnp.var(x, axis=axis, keepdims=True)
    return (x - m) / jnp.sqrt(v + eps)

def _scatter_add(tgt, idx, src, axis=0):
    return tgt.at[idx].add(src)

def _segment_sum(src, seg, n):
    return jax.ops.segment_sum(src, seg, n)
kernel_name = 'mk_decoder_postln_d1_seqx_r4_0f1b91'

def setup_inputs(seed: int=0):
    np.random.seed(seed)
    _w = jnp.asarray

    def _rec_inputs():
        import jax
        import jax.numpy as jnp
        _rk = jax.random.key(seed)
        x = 0.0001212 + 1 * jax.random.normal(jax.random.fold_in(_rk, 1), (16, 256, 512), jnp.float32)
        _lenS = 256 - jax.random.randint(jax.random.fold_in(_rk, 7), (16,), 0, max(1, 256 // 4) + 1, jnp.int32)
        _lenS2 = 256 - jax.random.randint(jax.random.fold_in(_rk, 8), (16,), 0, max(1, 256 // 4) + 1, jnp.int32)
        _ctx_2048P = jax.random.normal(jax.random.fold_in(_rk, 11), (16, 16, 512), jnp.float32)
        _ctx_2048c = jax.random.dirichlet(jax.random.fold_in(_rk, 511), 0.3 * jnp.ones((16,), jnp.float32), (16, 256))
        _ctx_2048t = jnp.einsum('bsk,bkd->bsd', _ctx_2048c, _ctx_2048P)
        _ctx_2048t = _ctx_2048t * jax.lax.rsqrt(jnp.mean(jnp.square(_ctx_2048t)) + 1e-12) * 0.953939
        ctx_2048 = 0.000173663 + 1.0001 * (_ctx_2048t + 0.3 * jax.random.normal(jax.random.fold_in(_rk, 611), (16, 256, 512), jnp.float32))
        return (x, ctx_2048)
    x, ctx_2048 = _rec_inputs()

    def _L0_attn_setup():
        import jax, jax.numpy as jnp
        import numpy as np
        H, HKV, HD = (16, 4, 128)

        def _rope(x, cos, sin):
            xr = x.reshape(*x.shape[:-1], HD // 2, 2)
            a, b = (xr[..., 0], xr[..., 1])
            c = cos[None, :, None, :]
            s = sin[None, :, None, :]
            return jnp.stack([a * c - b * s, a * s + b * c], axis=-1).reshape(x.shape)
        key = jax.random.key(seed)
        ks = jax.random.split(key, 5)
        B, T, C = (2, 512, 512)
        std = 0.02
        return {'x': jax.random.normal(ks[0], (B, T, C), jnp.float32), 'Wq': jax.random.normal(ks[1], (C, H * HD), jnp.float32) * std, 'bq': jnp.zeros((H * HD,), jnp.float32), 'Wk': jax.random.normal(ks[2], (C, HKV * HD), jnp.float32) * std, 'bk': jnp.zeros((HKV * HD,), jnp.float32), 'Wv': jax.random.normal(ks[3], (C, HKV * HD), jnp.float32) * std, 'bv': jnp.zeros((HKV * HD,), jnp.float32), 'Wo': jax.random.normal(ks[4], (H * HD, C), jnp.float32) * std, 'bo': jnp.zeros((C,), jnp.float32)}
    _L0_attn_all = _L0_attn_setup()
    _L0_attn_in = {k: v for k, v in _L0_attn_all.items() if k in ('Wq', 'bq', 'Wk', 'bk', 'Wv', 'bv', 'Wo', 'bo')}
    del _L0_attn_all

    def _L0_xattn_setup():
        import jax, jax.numpy as jnp
        import numpy as np
        B_DIM, T_DIM, C_DIM = (16, 256, 512)

        def _wkv(w, u, k, v):
            Bn, Tn, Cn = k.shape
            NEG_INF = jnp.float32(-1e+38)

            def step(carry, kv_t):
                p, q, o = carry
                kt, vt = kv_t
                no = jnp.maximum(o, u + kt)
                A = jnp.exp(o - no)
                E = jnp.exp(u + kt - no)
                y = (A * p + E * vt) / (A * q + E)
                no2 = jnp.maximum(w + o, kt)
                A2 = jnp.exp(w + o - no2)
                E2 = jnp.exp(kt - no2)
                return ((A2 * p + E2 * vt, A2 * q + E2, no2), y)
            init = (jnp.zeros((Bn, Cn), k.dtype), jnp.zeros((Bn, Cn), k.dtype), jnp.full((Bn, Cn), NEG_INF, k.dtype))
            kT = jnp.moveaxis(k, 1, 0)
            vT = jnp.moveaxis(v, 1, 0)
            _, yT = jax.lax.scan(step, init, (kT, vT))
            return jnp.moveaxis(yT, 0, 1)
        key = jax.random.key(seed)
        k1, k2, k3, k4 = jax.random.split(key, 4)
        w = -jnp.exp(jax.random.normal(k1, (C_DIM,), jnp.float32))
        u = jax.random.normal(k2, (C_DIM,), jnp.float32)
        k = jax.random.normal(k3, (B_DIM, T_DIM, C_DIM), jnp.float32)
        v = jax.random.normal(k4, (B_DIM, T_DIM, C_DIM), jnp.float32)
        return {'B': B_DIM, 'T': T_DIM, 'C': C_DIM, 'w': w, 'u': u, 'k': k, 'v': v}
    _L0_xattn_all = _L0_xattn_setup()
    _L0_xattn_in = {k: v for k, v in _L0_xattn_all.items() if k in ('w', 'u')}
    del _L0_xattn_all

    def _L0_ffn_setup():
        import jax, jax.numpy as jnp
        import numpy as np
        D_IN = 512
        D_OUT = 512
        RANK = 16
        N_EXPERTS = 16
        MAX_EXPERTS = 32
        ROUTER_HID = 64
        TOPK = 2
        ALPHA = 1.0

        def _forward(x, W, bias, rw1, rb1, rw2, rb2, A, B, gates):
            lead = x.shape[:-1]
            x_flat = x.reshape(-1, D_IN)
            n = x_flat.shape[0]
            feat = jax.lax.stop_gradient(x_flat)
            h = jax.nn.silu(feat @ rw1.T + rb1)
            logits = (h @ rw2.T + rb2)[:, :N_EXPERTS] + gates[None, :]
            topv, topi = jax.lax.top_k(logits, TOPK)
            sm = jax.nn.softmax(topv, axis=-1)
            rows = jnp.arange(n)[:, None]
            coeff = jnp.zeros_like(logits).at[rows, topi].set(sm)
            base = x_flat @ W.T + bias
            xa = jnp.einsum('ni,eri->ner', x_flat, A)
            wxa = xa * coeff[:, :, None]
            delta = jnp.einsum('ner,eor->no', wxa, B)
            out = base + ALPHA * delta
            return out.reshape(*lead, D_OUT)
        key = jax.random.key(seed)
        ks = jax.random.split(key, 10)
        s = 0.02
        x = jax.random.normal(ks[0], (4, 1024, D_IN), dtype=jnp.float32)
        W = jax.random.normal(ks[1], (D_OUT, D_IN), dtype=jnp.float32) * s
        bias = jax.random.normal(ks[2], (D_OUT,), dtype=jnp.float32) * s
        rw1 = jax.random.normal(ks[3], (ROUTER_HID, D_IN), dtype=jnp.float32) * s
        rb1 = jnp.zeros((ROUTER_HID,), dtype=jnp.float32)
        rw2 = jax.random.normal(ks[4], (MAX_EXPERTS, ROUTER_HID), dtype=jnp.float32) * s
        rb2 = jnp.zeros((MAX_EXPERTS,), dtype=jnp.float32)
        A = jax.random.normal(ks[5], (N_EXPERTS, RANK, D_IN), dtype=jnp.float32) * s
        B = jax.random.normal(ks[6], (N_EXPERTS, D_OUT, RANK), dtype=jnp.float32) * s
        gates = jnp.ones((N_EXPERTS,), dtype=jnp.float32)
        return {'x': x, 'W': W, 'bias': bias, 'rw1': rw1, 'rb1': rb1, 'rw2': rw2, 'rb2': rb2, 'A': A, 'B': B, 'gates': gates}
    _L0_ffn_all = _L0_ffn_setup()
    _L0_ffn_in = {k: v for k, v in _L0_ffn_all.items() if k in ('W', 'bias', 'rw1', 'rb1', 'rw2', 'rb2', 'A', 'B', 'gates')}
    del _L0_ffn_all
    return {'x': x, 'ctx_2048': ctx_2048, 'L0_attn_Wq': _L0_attn_in['Wq'], 'L0_attn_bq': _L0_attn_in['bq'], 'L0_attn_Wk': _L0_attn_in['Wk'], 'L0_attn_bk': _L0_attn_in['bk'], 'L0_attn_Wv': _L0_attn_in['Wv'], 'L0_attn_bv': _L0_attn_in['bv'], 'L0_attn_Wo': _L0_attn_in['Wo'], 'L0_attn_bo': _L0_attn_in['bo'], 'L0_xattn_w': _L0_xattn_in['w'], 'L0_xattn_u': _L0_xattn_in['u'], 'L0_ffn_W': _L0_ffn_in['W'], 'L0_ffn_bias': _L0_ffn_in['bias'], 'L0_ffn_rw1': _L0_ffn_in['rw1'], 'L0_ffn_rb1': _L0_ffn_in['rb1'], 'L0_ffn_rw2': _L0_ffn_in['rw2'], 'L0_ffn_rb2': _L0_ffn_in['rb2'], 'L0_ffn_A': _L0_ffn_in['A'], 'L0_ffn_B': _L0_ffn_in['B'], 'L0_ffn_gates': _L0_ffn_in['gates']}

def reference(x, ctx_2048, L0_attn_Wq, L0_attn_bq, L0_attn_Wk, L0_attn_bk, L0_attn_Wv, L0_attn_bv, L0_attn_Wo, L0_attn_bo, L0_xattn_w, L0_xattn_u, L0_ffn_W, L0_ffn_bias, L0_ffn_rw1, L0_ffn_rb1, L0_ffn_rw2, L0_ffn_rb2, L0_ffn_A, L0_ffn_B, L0_ffn_gates):
    import jax
    import jax.numpy as jnp

    def _L0_attn_ref(x, Wq, bq, Wk, bk, Wv, bv, Wo, bo):
        import jax, jax.numpy as jnp
        import numpy as np
        H, HKV, HD = (16, 4, 128)

        def _rope(x, cos, sin):
            xr = x.reshape(*x.shape[:-1], HD // 2, 2)
            a, b = (xr[..., 0], xr[..., 1])
            c = cos[None, :, None, :]
            s = sin[None, :, None, :]
            return jnp.stack([a * c - b * s, a * s + b * c], axis=-1).reshape(x.shape)
        B, T, C = x.shape
        G = H // HKV
        q = (x @ Wq + bq).reshape(B, T, H, HD)
        k = (x @ Wk + bk).reshape(B, T, HKV, HD)
        v = (x @ Wv + bv).reshape(B, T, HKV, HD)
        theta = 1.0 / 10000.0 ** (jnp.arange(0, HD, 2, dtype=jnp.float32) / HD)
        freqs = jnp.arange(T, dtype=jnp.float32)[:, None] * theta[None, :]
        cos, sin = (jnp.cos(freqs), jnp.sin(freqs))
        q = _rope(q, cos, sin)
        k = _rope(k, cos, sin)
        q = q.transpose(0, 2, 1, 3).reshape(B, G, HKV, T, HD)
        k = k.transpose(0, 2, 1, 3)
        v = v.transpose(0, 2, 1, 3)
        scale = 1.0 / np.sqrt(H).astype(np.float32)
        scores = jnp.einsum('bgjtd,bjsd->bgjts', q, k) * scale
        mask = jnp.tril(jnp.ones((T, T), dtype=bool))
        scores = jnp.where(mask[None, None, None], scores, -jnp.inf)
        wei = jax.nn.softmax(scores, axis=-1)
        out = jnp.einsum('bgjts,bjsd->bgjtd', wei, v)
        out = out.transpose(0, 3, 1, 2, 4).reshape(B, T, H * HD)
        return out @ Wo + bo

    def _L0_xattn_ref(B, T, C, w, u, k, v):
        import jax, jax.numpy as jnp
        import numpy as np
        B_DIM, T_DIM, C_DIM = (16, 256, 512)

        def _wkv(w, u, k, v):
            Bn, Tn, Cn = k.shape
            NEG_INF = jnp.float32(-1e+38)

            def step(carry, kv_t):
                p, q, o = carry
                kt, vt = kv_t
                no = jnp.maximum(o, u + kt)
                A = jnp.exp(o - no)
                E = jnp.exp(u + kt - no)
                y = (A * p + E * vt) / (A * q + E)
                no2 = jnp.maximum(w + o, kt)
                A2 = jnp.exp(w + o - no2)
                E2 = jnp.exp(kt - no2)
                return ((A2 * p + E2 * vt, A2 * q + E2, no2), y)
            init = (jnp.zeros((Bn, Cn), k.dtype), jnp.zeros((Bn, Cn), k.dtype), jnp.full((Bn, Cn), NEG_INF, k.dtype))
            kT = jnp.moveaxis(k, 1, 0)
            vT = jnp.moveaxis(v, 1, 0)
            _, yT = jax.lax.scan(step, init, (kT, vT))
            return jnp.moveaxis(yT, 0, 1)
        return _wkv(w, u, k, v)

    def _L0_ffn_ref(x, W, bias, rw1, rb1, rw2, rb2, A, B, gates):
        import jax, jax.numpy as jnp
        import numpy as np
        D_IN = 512
        D_OUT = 512
        RANK = 16
        N_EXPERTS = 16
        MAX_EXPERTS = 32
        ROUTER_HID = 64
        TOPK = 2
        ALPHA = 1.0

        def _forward(x, W, bias, rw1, rb1, rw2, rb2, A, B, gates):
            lead = x.shape[:-1]
            x_flat = x.reshape(-1, D_IN)
            n = x_flat.shape[0]
            feat = jax.lax.stop_gradient(x_flat)
            h = jax.nn.silu(feat @ rw1.T + rb1)
            logits = (h @ rw2.T + rb2)[:, :N_EXPERTS] + gates[None, :]
            topv, topi = jax.lax.top_k(logits, TOPK)
            sm = jax.nn.softmax(topv, axis=-1)
            rows = jnp.arange(n)[:, None]
            coeff = jnp.zeros_like(logits).at[rows, topi].set(sm)
            base = x_flat @ W.T + bias
            xa = jnp.einsum('ni,eri->ner', x_flat, A)
            wxa = xa * coeff[:, :, None]
            delta = jnp.einsum('ner,eor->no', wxa, B)
            out = base + ALPHA * delta
            return out.reshape(*lead, D_OUT)
        return _forward(x, W, bias, rw1, rb1, rw2, rb2, A, B, gates)
    x = _layernorm(x + _L0_attn_ref(x, L0_attn_Wq, L0_attn_bq, L0_attn_Wk, L0_attn_bk, L0_attn_Wv, L0_attn_bv, L0_attn_Wo, L0_attn_bo), axis=-1)
    x = _layernorm(x + _L0_xattn_ref(16, 256, 512, L0_xattn_w, L0_xattn_u, x, ctx_2048), axis=-1)
    x = _layernorm(x + _L0_ffn_ref(x, L0_ffn_W, L0_ffn_bias, L0_ffn_rw1, L0_ffn_rb1, L0_ffn_rw2, L0_ffn_rb2, L0_ffn_A, L0_ffn_B, L0_ffn_gates), axis=-1)
    return x

_drawn_inputs = setup_inputs


def setup_inputs(seed=0):
    import zlib

    import numpy as np

    out = dict(_drawn_inputs(seed))
    spreads = {'L0_attn_bq': (0.0, 0.8),
     'L0_attn_bk': (0.0, 0.8),
     'L0_attn_bv': (0.0, 0.1),
     'L0_attn_bo': (0.0, 0.1),
     'L0_ffn_rb1': (0.0, 0.8),
     'L0_ffn_rb2': (0.0, 0.8),
     'L0_ffn_gates': (1.0, 0.6)}
    factors = {'L0_ffn_bias': 3.144, 'L0_ffn_rw1': 8.0, 'L0_ffn_rw2': 8.0}
    for name, (base, spread) in spreads.items():
        noise = np.random.default_rng([zlib.crc32(name.encode()), seed]).standard_normal(out[name].shape)
        drawn = base * np.exp(spread * noise) if base else spread * noise
        out[name] = jnp.asarray(drawn.astype(out[name].dtype))
    for name, factor in factors.items():
        out[name] = (out[name] * factor).astype(out[name].dtype)
    return out
```

```python
import numpy as np

import concourse.bass as bass
from concourse import mybir
from contextlib import ExitStack

BATCH, T, C = 16, 256, 512
H, HKV, HD = 16, 4, 128
P = 128
KC = C // P
TT = T // P
HALVES = 2
HEADS = H // HALVES
JL = HKV // HALVES
GROUP = H // HKV
SLOTS = 2 * HEADS
TURNS = BATCH // 2
ALL = BATCH * HEADS
EXP, RANK, HID = 16, 16, 64
ER = EXP * RANK // P
EPS = 1e-5
NEG = -1e38
MASKED = -3e38
SCALE = 1.0 / float(np.sqrt(H))

L_ROPE, L_SUM, L_S, L_T, L_PT, L_PV, L_WO = 1, 2, 3, 4, 5, 6, 7
L_OTL = L_WO
L_Y = 12
L_TAIL = HEADS - 1 + L_WO + 1
X_LO = 2
FIRST = -HEADS

PEELED = (2, 3, 3)

UNITS = HEADS + TT + JL
Q_UNIT = [0, 1, 2, 3, 4, 6, 8, 10]
X_UNIT = {4: 5, 5: 7, 6: 9, 7: 11}
ROPES = HEADS + JL
Q_ROPE = [0, 1, 2, 3, 4, 6, 8, 9]
X_ROPE = {4: 5, 5: 7}


def decoder(nc, xt, xn, ctxt, wq, wk, wv, wo, bq, bk, bv, bo, wdec, ubon, wf, wa, wb, rw1, rw2,
            fbias, rb1, rb2, gates, cos_t, sin_t, mask_t, ident_t, iota_t, out):
    fp32, fr, u32 = mybir.dt.float32, mybir.dt.float32r, mybir.dt.uint32
    ALU, ACT = mybir.AluOpType, mybir.ActivationFunctionType

    ctx = ExitStack()
    with ctx:
        def sb(name, shape, dt=fp32):
            return ctx.enter_context(nc.sbuf_tensor(name, shape, dt))

        def sem(name):
            return ctx.enter_context(nc.semaphore(name))

        resid = nc.dram_tensor("resid", (BATCH, T, C), fp32, kind="Internal").ap()
        mixed = nc.dram_tensor("mixed", (BATCH, T, C), fp32, kind="Internal").ap()

        Wq = [sb(f"Wq{i}", [P, HEADS, KC, HD], fr) for i in "hl"]
        Wk = [sb(f"Wk{i}", [P, JL, KC, HD], fr) for i in "hl"]
        Wv = [sb(f"Wv{i}", [P, KC, JL * HD], fr) for i in "hl"]
        Wo = [sb(f"Wo{i}", [P, HEADS, C], fr) for i in "hl"]
        Bq = sb("Bq", [P, HALVES, HEADS])
        Bk = sb("Bk", [P, HALVES, JL])
        Bv = sb("Bv", [P, HALVES, JL])
        Cos = sb("Cos", [P, T])
        Sin = sb("Sin", [P, T])
        Mask = sb("Mask", [P, P + T])
        Ident = sb("Ident", [P, P])
        Wb = sb("Wb", [P, KC])
        Ub = sb("Ub", [P, KC])
        Bo = sb("Bo", [P, C])
        XR = sb("XR", [P, KC, T])
        X = [sb(f"X{i}", [P, 2, KC, T], fr) for i in "hl"]
        K = [sb(f"K{i}", [P, 2, JL, T], fr) for i in "hl"]
        V = [sb(f"V{i}", [P, 2, TT, JL * HD], fr) for i in "hl"]
        QB = sb("QB", [P, 2, T])
        SW = sb("SW", [P, 2, T])
        RC = sb("RC", [P, 2, T])
        RSN = sb("RSN", [P, 2, T])
        RF = sb("RF", [P, 2, T])
        Q = [sb(f"Q{i}", [P, 2, T], fr) for i in "hl"]
        S = sb("S", [P, 2, P + T])
        NM = sb("NM", [P, 2, TT])
        L = sb("L", [P, 2, TT])
        RL = sb("RL", [P, 2, TT])
        PT = [sb(f"PT{i}", [P, 2, P + T], fr) for i in "hl"]
        OT = [sb(f"OT{i}", [P, 2, T], fr) for i in "hl"]
        XN = sb("XN", [P, 2, TT, C])
        RO = sb("RO", [P, 2, TT, C])
        KVT = sb("KVT", [P, 2, KC, T])
        KT, VT = KVT[:, 0, :, :], KVT[:, 1, :, :]
        stage = KVT[:, :, :, :].rearrange("p a k t -> p (a k t)").rearrange("p (s n) -> p s n", s=4)
        MX = sb("MX", [P, KC, T + 1])
        PS = sb("PS", [P, KC, T + 1])
        QS = sb("QS", [P, KC, T + 1])
        A2 = sb("A2", [P, KC, T])
        E2 = sb("E2", [P, KC, T])
        AD = sb("AD", [P, KC, T])
        ED = sb("ED", [P, KC, T])
        EV = sb("EV", [P, KC, T])
        ST = sb("ST", [P, 2, TT, 6])
        MV = sb("MV", [P, 2, TT, 2])
        VE = sb("VE", [P, 2, TT])
        RS = sb("RS", [P, 2, TT])
        ST2 = sb("ST2", [P, 2, TT, 6])
        MV2 = sb("MV2", [P, 2, TT, 2])
        VE2 = sb("VE2", [P, 2, TT])
        RS2 = sb("RS2", [P, 2, TT])
        Mhalf = sb("Mhalf", [P, TT])

        wq_flat = [w[:, :, :, :].rearrange("p h k n -> p (h k n)") for w in Wq]
        Wf = [w[:, 0:KC * C].rearrange("p (k n) -> p k n", k=KC) for w in wq_flat]
        Wa = [w[:, KC * C:KC * C + KC * EXP * RANK].rearrange("p (k n) -> p k n", k=KC) for w in wq_flat]
        Wd = [w[:, 3072:4096].rearrange("p (k n) -> p k n", k=ER) for w in wq_flat]
        Wr = [w[:, 0, :, :] for w in Wk]
        X2B = [b[:, :, :].rearrange("p k t -> p (k t)").rearrange("p (a c) -> p a c", a=TT) for b in (AD, ED)]
        WX = QB[:, :, :]
        WT = [a[:, :, :] for a in Q]
        HE, HS = RC[0:HID, 0, :], RC[0:HID, 1, :]
        Fb = Bo
        small = sb("small", [P, 96])
        Rw2, Rb1, NRb1 = small[0:HID, 0:16], small[0:HID, 16:17], small[0:HID, 17:18]
        Rb2, Gates, Iota = small[:, 32:48], small[:, 48:64], small[:, 64:80]
        s_flat = S[:, :, :].rearrange("p a n -> p (a n)")
        cut = lambda at, n, k: s_flat[:, at:at + n].rearrange("p (a k) -> p a k", k=k)
        LG0, LG1, LG = cut(0, 32, EXP), cut(32, 32, EXP), cut(64, 32, EXP)
        M8, I8 = cut(96, 16, 8), cut(112, 16, 8)
        IX = cut(128, 16, 8).bitcast(u32)
        DM, EM, SE, P1, P2 = (cut(144 + 2 * k, 2, 1) for k in range(5))
        C1, C2, CF = cut(160, 32, EXP), cut(192, 32, EXP), cut(224, 32, EXP)

        bank = [ctx.enter_context(nc.psum_tensor(f"bank{i}", [P, 512], fp32)) for i in range(8)]
        proj_ps = bank[0:2]
        s_ps, pt_ps, ot_ps, tail_ps = bank[2], bank[3], bank[4], bank[7]
        acc_ps = bank[5:7]

        const_in = sem("const_in")
        stage_in = [sem(f"stage_in{i}") for i in range(4)]
        w_hi, w_lo = sem("w_hi"), sem("w_lo")
        consts = sem("consts")
        x_in, x_hi, x_lo = sem("x_in"), sem("x_hi"), sem("x_lo")
        n_in, r_out = ([sem(f"{n}{i}") for i in range(2)] for n in ("n_in", "r_out"))
        n_sum = sem("n_sum")
        projected, evacuated, v_lo = sem("projected"), sem("evacuated"), sem("v_lo")
        swapped = [sem(f"swapped{i}") for i in range(2)]
        rotated, summed = sem("rotated"), sem("summed")
        rope_hi, rope_lo = sem("rope_hi"), sem("rope_lo")
        scored, maxed, exped, inverted, normed = (sem(n) for n in ("scored", "maxed", "exped", "inverted", "normed"))
        turned, pt_hi, pt_lo = sem("turned"), sem("pt_hi"), sem("pt_lo")
        mixed_v, ot_hi, ot_lo, wo_done = sem("mixed_v"), sem("ot_hi"), sem("ot_lo"), sem("wo_done")
        acc_read = sem("acc_read")
        x1_ve, x1_rs, x1_done = sem("x1_ve"), sem("x1_rs"), sem("x1_done")
        x1_turned, kt_copied = sem("x1_turned"), sem("kt_copied")
        v_in = sem("v_in")
        mx_done, a2_arg, e2_arg, a2_done, e2_done = (sem(n) for n in ("mx_done", "a2_arg", "e2_arg", "a2_done", "e2_done"))
        d_done, ed_arg, ad_arg, ad_done, ed_done = (sem(n) for n in ("d_done", "ed_arg", "ad_arg", "ad_done", "ed_done"))
        e2v_done, ev_done, qs_done, ps_done = sem("e2v_done"), sem("ev_done"), sem("qs_done"), sem("ps_done")
        aq_done, den_done, pairs_done, quad_done = (sem(n) for n in ("aq_done", "den_done", "pairs_done", "quad_done"))
        rquad_done, rden_done, cross_done = sem("rquad_done"), sem("rden_done"), sem("cross_done")
        ap_done, num_done, y_done = sem("ap_done"), sem("num_done"), sem("y_done")
        y_turned, x2_sum, x2_ve, x2_rs, x2_done = (sem(n) for n in ("y_turned", "x2_sum", "x2_ve", "x2_rs", "x2_done"))
        x2_out = [sem(f"x2_out{i}") for i in range(2)]

        f_in = [sem(f"f_in{i}") for i in range(2)]
        f_const, fb_in = sem("f_const"), sem("fb_in")
        f_turned, xt_hi, xt_lo, biased, f_ready = (sem(n) for n in ("f_turned", "xt_hi", "xt_lo", "biased", "f_ready"))
        hid_done, hid_exp, hid_1p, hid_inv, silu_done = (sem(n) for n in ("hid_done", "hid_exp", "hid_1p", "hid_inv", "silu_done"))
        low_done, logits_done, lg_b, lg_g, lg_sum = (sem(n) for n in ("low_done", "logits_done", "lg_b", "lg_g", "lg_sum"))
        top_diff, top_exp, top_sum, top_p1, top_p2 = (sem(n) for n in ("top_diff", "top_exp", "top_sum", "top_p1", "top_p2"))
        coef_parts, coef_done, weighted = sem("coef_parts"), sem("coef_done"), sem("weighted")
        wt_turned, wt_hi, wt_lo, f_mm, f_sum = (sem(n) for n in ("wt_turned", "wt_hi", "wt_lo", "f_mm", "f_sum"))
        f_ve, f_rs, f_done = sem("f_ve"), sem("f_rs"), sem("f_done")
        f_out = [sem(f"f_out{i}") for i in range(2)]

        def live(it, n, lag, step=1):
            if (n - lag) % step:
                return False
            return not isinstance(it, int) or 0 <= it * SLOTS + n - lag < ALL

        def head(hf, it, n, lag):
            return it * SLOTS + (hf * ALL + n - lag)

        def batch(hf, it, n, lag):
            return it * 2 + (hf * BATCH + (n - lag) // HEADS)

        def pair(hf, it, n, lag):
            return it + ((hf * BATCH + (n - lag) // HEADS) // 2 + 1)

        def numbered(hf, it, k, per, before, q_order, x_order):
            m, q = k % HEADS, q_order is not None
            if isinstance(it, int) and it * SLOTS + k < 0:
                at = sorted(x_order).index(m)
                return hf * BATCH * per + at, at % 2, (hf * BATCH * per + at) // 2 + 1
            last = isinstance(it, int) and it * 2 + k // HEADS == BATCH - 1
            at = (m if last else q_order[m]) if q else x_order[m]
            at += hf * BATCH * per + (k // HEADS) * per + before
            return it * (2 * per) + at, at % 2, it * per + (at // 2 + 1)

        def unit_q(hf, it, k):
            return numbered(hf, it, k, UNITS, TT + JL, Q_UNIT, None)

        def unit_x(hf, it, k):
            return numbered(hf, it, k, UNITS, TT + JL, None, X_UNIT)

        def rope_q(hf, it, k):
            return numbered(hf, it, k, ROPES, JL, Q_ROPE, None)

        def rope_x(hf, it, k):
            return numbered(hf, it, k, ROPES, JL, None, X_ROPE)

        def above(eng, s, value):
            assert isinstance(value, int) or value.min_val > 0
            if not isinstance(value, int) or value > 0:
                eng.wait_ge(s, value)

        def more(it, n):
            return not isinstance(it, int) or 0 <= it * 2 + n // HEADS + 1 < BATCH

        def extra(it, n):
            m = n % HEADS
            if m < 4 or not more(it, n):
                return None
            par = (n // HEADS + 1) % 2
            return ("K", m - 4, par) if m < 6 else ("V", m - 6, par)

        def run_slots(eng, slot, trailing):
            for hf in range(HALVES):
                peeled = PEELED[hf]
                for n in range(FIRST, peeled * SLOTS):
                    slot(hf, 0, n)
                with eng.Fori(peeled, TURNS - 1) as it:
                    for n in range(SLOTS):
                        slot(hf, it, n)
                for n in range(SLOTS + trailing[hf]):
                    slot(hf, TURNS - 1, n)

        def pieces(hf):
            for kc in range(0, KC, 2):
                yield [w[:, kc:kc + 2, :].rearrange("p k n -> p (k n)") for w in Wv], wv[hf, :, kc:kc + 2, :].rearrange("p k n -> p (k n)")
            for j in range(JL):
                yield [w[:, j, :, :].rearrange("p k n -> p (k n)") for w in Wk], wk[hf, :, j, :, :].rearrange("p k n -> p (k n)")
            for h in range(HEADS):
                yield [w[:, h, :, :].rearrange("p k n -> p (k n)") for w in Wq], wq[hf, :, h, :, :].rearrange("p k n -> p (k n)")
            for h in range(HEADS):
                yield [w[:, h, :] for w in Wo], wo[hf, :, h, :]
        def ffn_pieces():
            yield [w.rearrange("p k n -> p (k n)") for w in Wr], rw1.rearrange("p k n -> p (k n)")
            for k in range(0, KC, 2):
                yield [w[:, k:k + 2, :].rearrange("p k n -> p (k n)") for w in Wa], wa[:, k:k + 2, :].rearrange("p k n -> p (k n)")
            for k in range(KC):
                yield [w[:, k, :] for w in Wf], wf[:, k, :]
            for k in range(ER):
                yield [w[:, k, :] for w in Wd], wb[:, k, :]

        def run_steps(eng, step, trailing):
            for n in range(2 * PEELED[2]):
                step(0, n)
            with eng.Fori(PEELED[2], TURNS) as it:
                for n in range(2):
                    step(it, n)
            for n in range(trailing):
                step(TURNS, n)

        def stage_live(it, n, lag):
            return not isinstance(it, int) or 0 <= it * 2 + n - lag < BATCH

        PIECES = [list(pieces(hf)) for hf in range(HALVES)]
        NP = len(PIECES[0])
        FFN = list(ffn_pieces())
        CONSTS = [(Bq, bq), (Bk, bk), (Bv, bv), (Cos, cos_t), (Sin, sin_t), (Mask, mask_t),
                  (Ident, ident_t), (Wb, wdec), (Ub, ubon), (Bo, bo), (Iota, iota_t),
                  (Rb2, rb2), (Gates, gates), (Rw2, rw2), (Rb1, rb1)]

        def rotations(hf, it, n):
            found = []
            k = n - L_SUM
            if live(it, n, L_SUM):
                found.append((*rope_q(hf, it, k), [a[:, k % 2, :] for a in Q], head(hf, it, k, 0) - 1))
            e = extra(it, k)
            if e and e[0] == "K":
                found.append((*rope_x(hf, it, k), [a[:, e[2], e[1], :] for a in K],
                              it * SLOTS + (hf * ALL + k // HEADS * HEADS)))
            return found

        block = ctx.enter_context(nc.Block())

        @block.sync
        def _(sp):
            for dst, src in CONSTS:
                sp.dma_start(dst[tuple(slice(None) for _ in dst.shape)], src).then_inc(const_in, 16)

            def slot(hf, it, n):
                m = n % HEADS
                if m == 0 and more(it, n):
                    b = it * 2 + (n // HEADS + 1)
                    above(sp, x_lo, b + hf * BATCH)
                    sp.dma_start(XR[:, :, :], xt[b, :, :, :]).then_inc(x_in, 16)
                if live(it, n, 0):
                    r = rope_q(hf, it, n)[1]
                    sp.wait_ge(evacuated, unit_q(hf, it, n)[0] + 1)
                    sp.dma_start(SW[0:64, r, :], QB[64:128, r, :]).then_inc(swapped[r], 16)
                    sp.dma_start(SW[64:128, r, :], QB[0:64, r, :]).then_inc(swapped[r], 16)
                e = extra(it, n)
                if e and e[0] == "K":
                    r = rope_x(hf, it, n)[1]
                    sp.wait_ge(evacuated, unit_x(hf, it, n)[0] + 1)
                    sp.dma_start(SW[0:64, r, :], QB[64:128, r, :]).then_inc(swapped[r], 16)
                    sp.dma_start(SW[64:128, r, :], QB[0:64, r, :]).then_inc(swapped[r], 16)
                if live(it, n, 4, HEADS):
                    par = ((n - 4) // HEADS) % 2
                    b = batch(0, it, n, 4)
                    above(sp, acc_read, batch(hf, it, n, 4) - 1)
                    sp.dma_start(XN[:, par, :, :], (xn if hf == 0 else resid)[b, :, :].rearrange("(a p) c -> p a c", p=P)).then_inc(n_in[par], 16)
                if hf == 0 and live(it, n, L_TAIL + 1, HEADS):
                    par = ((n - L_TAIL - 1) // HEADS) % 2
                    b = batch(0, it, n, L_TAIL + 1)
                    sp.wait_ge(acc_read, b + 1)
                    sp.dma_start(resid[b, :, :].rearrange("(a p) c -> p a c", p=P), RO[:, par, :, :]).then_inc(r_out[par], 16)
                if hf == 1 and live(it, n, L_TAIL + 2, HEADS):
                    b = batch(0, it, n, L_TAIL + 2)
                    above(sp, ev_done, b)
                    sp.dma_start(VT[:, :, :], ctxt[b, :, :, :]).then_inc(v_in, 16)
                if hf == 1 and live(it, n, L_TAIL + 15, HEADS):
                    par = ((n - L_TAIL - 14) // HEADS) % 2
                    b = batch(0, it, n, L_TAIL + 15)
                    sp.wait_ge(x2_done, b + 1)
                    sp.dma_start(mixed[b, :, :].rearrange("(a p) c -> p a c", p=P), RO[:, par, :, :]).then_inc(x2_out[par], 16)

            for hf in range(HALVES):
                if hf == 1:
                    sp.wait_ge(wo_done, ALL)
                    for i in range(2):
                        sp.wait_ge(r_out[i], 16 * BATCH // 2)
                for i, (_, src) in enumerate(PIECES[hf]):
                    u = hf * NP + i
                    if u >= 4:
                        sp.wait_ge(w_lo, u - 3)
                    sp.dma_start(stage[:, u % 4, :], src).then_inc(stage_in[u % 4], 16)
                    if i == 0:
                        slot(hf, 0, FIRST)
                peeled = PEELED[hf]
                for n in range(FIRST + 1, peeled * SLOTS):
                    slot(hf, 0, n)
                with sp.Fori(peeled, TURNS - 1) as it:
                    for n in range(SLOTS):
                        slot(hf, it, n)
                for n in range(SLOTS + L_TAIL + 17):
                    slot(hf, TURNS - 1, n)
            for i in range(2):
                sp.wait_ge(x2_out[i], 16 * BATCH // 2)
            sp.dma_start(Fb[:, :], fbias).then_inc(fb_in, 16)
            for i, (_, src) in enumerate(FFN):
                u = 2 * NP + i
                sp.wait_ge(w_lo, u - 3)
                sp.dma_start(stage[:, u % 4, :], src).then_inc(stage_in[u % 4], 16)

            def step(it, n):
                if stage_live(it, n, 0):
                    b = it * 2 + n
                    above(sp, biased, b - 1)
                    sp.dma_start(XN[:, n % 2, :, :], mixed[b, :, :].rearrange("(a p) c -> p a c", p=P)).then_inc(f_in[n % 2], 16)
                if stage_live(it, n, 4):
                    b = it * 2 + (n - 4)
                    sp.wait_ge(f_done, b + 1)
                    sp.dma_start(out[b, :, :].rearrange("(a p) c -> p a c", p=P), RO[:, n % 2, :, :]).then_inc(f_out[n % 2], 16)

            run_steps(sp, step, 4)
            for i in range(2):
                sp.wait_ge(f_out[i], 16 * BATCH // 2)
        @block.tensor
        def _(pe):
            def three(dst, lhs, rhs, first=True, last=True):
                nc.tensor.matmul(dst, lhs[0], rhs[0], start=first, stop=False)
                nc.tensor.matmul(dst, lhs[0], rhs[1], start=False, stop=False)
                return nc.tensor.matmul(dst, lhs[1], rhs[0], start=False, stop=last)

            def slot(hf, it, n):
                m = n % HEADS
                if live(it, n, L_S):
                    g, i = head(hf, it, n, L_S), (n - L_S) % SLOTS
                    par, j, q = i // HEADS, (i % HEADS) // GROUP, i % 2
                    pe.wait_ge(rope_lo, rope_q(hf, it, n - L_S)[0] + 1)
                    above(pe, maxed, g)
                    for t, c0, keys in ((0, 0, P), (1, P, T)):
                        last = three(s_ps[:, c0:c0 + keys], [a[:, q, t * P:(t + 1) * P] for a in Q],
                                     [a[:, par, j, 0:keys] for a in K])
                    last.then_inc(scored, 1)
                if live(it, n, 0):
                    u, place, _ = unit_q(hf, it, n)
                    par = (n // HEADS) % 2
                    if isinstance(it, int) and it == 0 and n < HEADS:
                        pe.wait_ge(w_lo, hf * NP + TT + JL + m + 1)
                    if m == 1:
                        pe.wait_ge(v_lo, it * (2 * TT) + (hf * BATCH + n // HEADS + 1) * TT)
                    above(pe, evacuated, u - 1)
                    dst = proj_ps[place][:, 0:T]
                    for kc in range(KC):
                        last = three(dst, [w[:, m, kc, :] for w in Wq], [x[:, par, kc, :] for x in X],
                                     kc == 0, kc == KC - 1)
                    last.then_inc(projected, 1)
                if live(it, n, L_PV):
                    g, i = head(hf, it, n, L_PV), (n - L_PV) % SLOTS
                    par, j = i // HEADS, (i % HEADS) // GROUP
                    pe.wait_ge(pt_lo, g + 1)
                    if i % HEADS == 0:
                        pe.wait_ge(v_lo, (batch(hf, it, n, L_PV) + 1) * TT)
                    above(pe, ot_lo, g)
                    vs = [[v[:, par, t, j * HD:(j + 1) * HD] for v in V] for t in range(TT)]
                    three(ot_ps[:, 0:T], vs[0], [a[:, i % 2, 0:T] for a in PT], True, False)
                    three(ot_ps[:, P:T], vs[1], [a[:, i % 2, T:T + P] for a in PT], False, True).then_inc(mixed_v, 1)
                e = extra(it, n)
                if e:
                    kind, tile, par = e
                    u, place, _ = unit_x(hf, it, n)
                    dst = proj_ps[place][:, 0:T]
                    nb = it * 2 + (hf * BATCH + n // HEADS + 1)
                    if m == 4:
                        pe.wait_ge(x_lo, nb + 1)
                        if isinstance(it, int) and n < 0:
                            pe.wait_ge(w_lo, hf * NP + TT + JL)
                    if m == 7:
                        pe.wait_ge(v_lo, nb * TT + 1)
                    above(pe, evacuated, u - 1)
                    for kc in range(KC):
                        if kind == "V":
                            last = three(dst, [x[:, par, kc, tile * P:(tile + 1) * P] for x in X],
                                         [w[:, kc, :] for w in Wv], kc == 0, kc == KC - 1)
                        else:
                            last = three(dst, [w[:, tile, kc, :] for w in Wk],
                                         [x[:, par, kc, :] for x in X], kc == 0, kc == KC - 1)
                    last.then_inc(projected, 1)
                if live(it, n, L_WO):
                    g, i = head(hf, it, n, L_WO), (n - L_WO) % SLOTS
                    h = i % HEADS
                    pe.wait_ge(ot_lo, g + 1)
                    if isinstance(it, int) and it == 0 and n - L_WO < HEADS:
                        pe.wait_ge(w_lo, hf * NP + TT + JL + HEADS + h + 1)
                    if h == 0:
                        above(pe, acc_read, batch(hf, it, n, L_WO))
                    for t in range(TT):
                        last = three(acc_ps[t][:, :], [a[:, i % 2, t * P:(t + 1) * P] for a in OT],
                                     [w[:, h, :] for w in Wo], h == 0, h == HEADS - 1)
                    last.then_inc(wo_done, 1)
                if hf == 1:
                    for t in range(TT):
                        if live(it, n, L_TAIL + 2 + t, HEADS):
                            turn_x1(hf, it, n, t)
                        if live(it, n, L_TAIL + L_Y + t, HEADS):
                            turn_y(hf, it, n, t)
                if live(it, n, L_T):
                    g, i = head(hf, it, n, L_T), (n - L_T) % SLOTS
                    pe.wait_ge(normed, g + 1)
                    above(pe, pt_lo, g)
                    for k in range(3):
                        last = nc.tensor.transpose(pt_ps[:, k * P:(k + 1) * P], S[:, i % 2, k * P:(k + 1) * P], Ident[:, :])
                    last.then_inc(turned, 1)

            def turn_x1(hf, it, n, t):
                b = batch(0, it, n, L_TAIL + 2 + t)
                par = ((n - L_TAIL - 2 - t) // HEADS) % 2
                pe.wait_ge(x1_done, b + 1)
                if t == 0:
                    above(pe, x2_sum, TT * (b - 1))
                else:
                    pe.wait_ge(kt_copied, TT * b + t)
                for c in range(KC):
                    last = nc.tensor.transpose(tail_ps[:, c * P:(c + 1) * P], RO[:, par, t, c * P:(c + 1) * P], Ident[:, :])
                last.then_inc(x1_turned, 1)

            def turn_y(hf, it, n, t):
                b = batch(0, it, n, L_TAIL + L_Y + t)
                pe.wait_ge(y_done, b + 1)
                if t == 0:
                    if isinstance(it, int):
                        pe.wait_ge(kt_copied, TT * min(b + 2, BATCH))
                    else:
                        pe.wait_ge(kt_copied, TT * b + 2 * TT)
                else:
                    pe.wait_ge(x2_sum, TT * b + t)
                for c in range(KC):
                    last = nc.tensor.transpose(tail_ps[:, c * P:(c + 1) * P], EV[:, c, t * P:(t + 1) * P], Ident[:, :])
                last.then_inc(y_turned, 1)

            pe.wait_ge(const_in, 16 * len(CONSTS))
            run_slots(pe, slot, (L_TAIL, L_TAIL + 17))

            def step(it, n):
                def dense(t):
                    if stage_live(it, n, 3):
                        b, par = it * 2 + (n - 3), (n - 3) % 2
                        if t == 0:
                            pe.wait_ge(wt_lo, b + 1)
                        above(pe, f_sum, TT * (b - 1) + (t + 1))
                        for k in range(KC):
                            three(bank[5 + t][:, :], [x[:, par, k, t * P:(t + 1) * P] for x in X], [w[:, k, :] for w in Wf], k == 0, False)
                        for r in range(ER):
                            last = three(bank[5 + t][:, :], [a[:, r, t * P:(t + 1) * P] for a in WT], [w[:, r, :] for w in Wd], False, r == ER - 1)
                        last.then_inc(f_mm, 1)

                dense(0)
                if stage_live(it, n, 2):
                    b, par = it * 2 + (n - 2), n % 2
                    xs = lambda k, c: [x[:, par, k, c] for x in X]
                    pe.wait_ge(xt_lo, TT * b + TT)
                    above(pe, silu_done, b)
                    for k in range(KC):
                        last = three(bank[2][:, 0:T], [w[:, k, :] for w in Wr], xs(k, slice(0, T)), k == 0, k == KC - 1)
                    last.then_inc(hid_done, 1)
                    above(pe, weighted, b)
                    for t in range(TT):
                        for k in range(KC):
                            last = three(bank[3][:, t * T:(t + 1) * T], xs(k, slice(t * P, (t + 1) * P)),
                                         [w[:, k, :] for w in Wa], k == 0, k == KC - 1)
                    last.then_inc(low_done, 1)
                if stage_live(it, n, 2):
                    b = it * 2 + (n - 2)
                    pe.wait_ge(silu_done, b + 1)
                    above(pe, lg_b, b)
                    for a in range(TT):
                        last = nc.tensor.matmul(bank[4][:, a * EXP:(a + 1) * EXP], HS[:, a * P:(a + 1) * P], Rw2, start=True, stop=True)
                    last.then_inc(logits_done, 1)
                dense(1)
                if stage_live(it, n, 1):
                    b, par = it * 2 + (n - 1), (n - 1) % 2
                    pe.wait_ge(f_in[par], (it + ((n - 1) // 2 + 1)) * 16)
                    for t in range(TT):
                        above(pe, xt_lo, TT * b + (t - 1))
                        for c in range(KC):
                            last = nc.tensor.transpose(bank[t][:, c * P:(c + 1) * P], XN[:, par, t, c * P:(c + 1) * P], Ident[:, :])
                        last.then_inc(f_turned, 1)
                if stage_live(it, n, 2):
                    b = it * 2 + (n - 2)
                    pe.wait_ge(weighted, b + 1)
                    above(pe, wt_lo, b)
                    for r in range(ER):
                        for t in range(TT):
                            last = nc.tensor.transpose(bank[7][:, r * T + t * P:r * T + (t + 1) * P], WX[:, t, r * P:(r + 1) * P], Ident[:, :])
                    last.then_inc(wt_turned, 1)

            pe.wait_ge(w_lo, 2 * NP + len(FFN))
            run_steps(pe, step, 3)

        @block.scalar
        def _(act):
            def copy(dst, src, **kw):
                return nc.scalar.activation(dst, src, ACT.Copy, **kw)

            def evacuate(hf, it, n, unit, rope, bias, kind=None):
                u, place, _ = unit(hf, it, n)
                q = proj_ps[place][:, 0:T]
                act.wait_ge(projected, u + 1)
                if kind is not None:
                    tile, par = kind
                    nb = it * 2 + (hf * BATCH + n // HEADS + 1)
                    above(act, mixed_v, nb * HEADS - HEADS)
                    copy(V[0][:, par, tile, :], q).then_inc(evacuated, 1)
                    return
                r, rp, _ = rope(hf, it, n)
                above(act, rotated, r - 1)
                nc.scalar.activation(QB[:, rp, :], q, ACT.Identity, bias=bias).then_inc(evacuated, 1)

            def slot(hf, it, n):
                m = n % HEADS
                if live(it, n, L_PT):
                    g, i = head(hf, it, n, L_PT), (n - L_PT) % 2
                    act.wait_ge(turned, g + 1)
                    above(act, mixed_v, g - 1)
                    copy(PT[0][:, i, :], pt_ps[:, 0:P + T]).then_inc(pt_hi, 1)
                if m == 1 and more(it, n):
                    nb = it * 2 + (hf * BATCH + n // HEADS + 1)
                    act.wait_ge(x_in, 16 * nb + 16)
                    if not isinstance(it, int) or it * 2 + n // HEADS - 1 >= 0:
                        act.wait_ge(projected, unit_q(hf, it, n // HEADS * HEADS - 1)[0] + 1)
                    copy(X[0][:, (n // HEADS + 1) % 2, :, :], XR[:, :, :]).then_inc(x_hi, 1)
                for r, rp, _, dst, used in rotations(hf, it, n):
                    act.wait_ge(summed, r + 1)
                    above(act, scored, used)
                    copy(dst[0], RF[:, rp, :]).then_inc(rope_hi, 1)
                if live(it, n, L_S):
                    g, i = head(hf, it, n, L_S), (n - L_S) % 2
                    act.wait_ge(maxed, g + 1)
                    for t, c in ((0, slice(0, P)), (1, slice(P, P + T))):
                        last = nc.scalar.activation(S[:, i, c], S[:, i, c], ACT.Exp, bias=NM[:, i, t:t + 1],
                                                    scale=-1.0, accum_out=L[:, i, t:t + 1])
                    last.then_inc(exped, 1)
                if live(it, n, 0):
                    evacuate(hf, it, n, unit_q, rope_q, Bq[:, hf, m:m + 1])
                if live(it, n, L_PV):
                    g, i = head(hf, it, n, L_PV), (n - L_PV) % SLOTS
                    act.wait_ge(mixed_v, g + 1)
                    above(act, wo_done, g - 1)
                    j = (i % HEADS) // GROUP
                    nc.scalar.activation(OT[0][:, i % 2, :], ot_ps[:, 0:T], ACT.Identity,
                                         bias=Bv[:, hf, j:j + 1]).then_inc(ot_hi, 1)
                e = extra(it, n)
                if e:
                    kind, tile, par = e
                    if kind == "V":
                        evacuate(hf, it, n, unit_x, None, None, (tile, par))
                    else:
                        evacuate(hf, it, n, unit_x, rope_x, Bk[:, hf, tile:tile + 1])
                if hf == 1:
                    tail(it, n, 0)
                if live(it, n, L_S):
                    g, i = head(hf, it, n, L_S), (n - L_S) % 2
                    act.wait_ge(inverted, g + 1)
                    copy(S[:, i, 0:P], S[:, i, 0:P], scale=RL[:, i, 0:1])
                    copy(S[:, i, P:P + T], S[:, i, P:P + T], scale=RL[:, i, 1:2]).then_inc(normed, 1)
                if hf == 1:
                    tail(it, n, 1)

            def tail(it, n, part):
                def at(lag, p):
                    return part == p and live(it, n, L_TAIL + lag, HEADS)

                for t in range(TT):
                    if at((3 if t == 0 else 3), 1):
                        b = batch(0, it, n, L_TAIL + (3 if t == 0 else 3))
                        act.wait_ge(x1_turned, TT * b + t + 1)
                        above(act, d_done, b)
                        above(act, e2_arg, b)
                        copy(KT[:, :, t * P:(t + 1) * P], tail_ps[:, :].rearrange("p (c t) -> p c t", c=KC)).then_inc(kt_copied, 1)
                if at(5, 1):
                    b = batch(0, it, n, L_TAIL + 5)
                    act.wait_ge(a2_arg, b + 1)
                    nc.scalar.activation(A2[:, :, :], A2[:, :, :], ACT.Exp).then_inc(a2_done, 1)
                if at(6, 0):
                    b = batch(0, it, n, L_TAIL + 6)
                    act.wait_ge(e2_arg, b + 1)
                    nc.scalar.activation(E2[:, :, :], E2[:, :, :], ACT.Exp).then_inc(e2_done, 1)
                if at(6, 1):
                    b = batch(0, it, n, L_TAIL + 6)
                    act.wait_ge(ad_arg, b + 1)
                    nc.scalar.activation(AD[:, :, :], AD[:, :, :], ACT.Exp).then_inc(ad_done, 1)
                if at(7, 0):
                    b = batch(0, it, n, L_TAIL + 7)
                    act.wait_ge(ed_arg, b + 1)
                    nc.scalar.activation(ED[:, :, :], ED[:, :, :], ACT.Exp).then_inc(ed_done, 1)

            act.wait_ge(const_in, 16 * len(CONSTS))
            for hf in range(HALVES):
                def weight(i):
                    u = hf * NP + i
                    act.wait_ge(stage_in[u % 4], 16 * (u // 4 + 1))
                    copy(PIECES[hf][i][0][0], stage[:, u % 4, :]).then_inc(w_hi, 1)
                for i in range(NP):
                    weight(i)
                    if i == TT + JL:
                        slot(hf, 0, FIRST)
                        slot(hf, 0, FIRST + 1)
                peeled = PEELED[hf]
                for n in range(FIRST + 2, peeled * SLOTS):
                    slot(hf, 0, n)
                with act.Fori(peeled, TURNS - 1) as it:
                    for n in range(SLOTS):
                        slot(hf, it, n)
                for n in range(SLOTS + (L_TAIL, L_TAIL + 17)[hf]):
                    slot(hf, TURNS - 1, n)

            def step(it, n):
                if stage_live(it, n, 3):
                    b = it * 2 + (n - 3)
                    act.wait_ge(wt_turned, b + 1)
                    above(act, f_mm, TT * b)
                    copy(WT[0][:, :, :], bank[7][:, :].rearrange("p (r t) -> p r t", r=ER)).then_inc(wt_hi, 1)
                if stage_live(it, n, 2):
                    b, par = it * 2 + (n - 2), (n - 2) % 2
                    above(act, f_mm, TT * (b - 1))
                    for t in range(TT):
                        act.wait_ge(f_turned, TT * b + (t + 1))
                        copy(X[0][:, par, :, t * P:(t + 1) * P], bank[t][:, :].rearrange("p (c t) -> p c t", c=KC)).then_inc(xt_hi, 1)
                if stage_live(it, n, 2):
                    b = it * 2 + (n - 2)
                    act.wait_ge(hid_done, b + 1)
                    above(act, hid_1p, b)
                    nc.scalar.activation(HE, bank[2][0:HID, 0:T], ACT.Exp, bias=NRb1, scale=-1.0).then_inc(hid_exp, 1)
                    act.wait_ge(top_diff, b + 1)
                    nc.scalar.activation(EM, DM, ACT.Exp).then_inc(top_exp, 1)

            for i, ((hi, _), _) in enumerate(FFN):
                u = 2 * NP + i
                act.wait_ge(stage_in[u % 4], 16 * (u // 4 + 1))
                copy(hi, stage[:, u % 4, :]).then_inc(w_hi, 1)
            run_steps(act, step, 3)

        @block.gpsimd
        def _(pool):
            gp = nc.gpsimd

            def rotate(r, rp, nth):
                pool.wait_ge(swapped[rp], nth * 32)
                above(pool, summed, r - 1)
                gp.tensor_tensor(RC[:, rp, :], QB[:, rp, :], Cos[:, :], ALU.mult)
                gp.tensor_tensor(RSN[:, rp, :], SW[:, rp, :], Sin[:, :], ALU.mult).then_inc(rotated, 1)

            def slot(hf, it, n):
                if live(it, n, L_ROPE):
                    rotate(*rope_q(hf, it, n - L_ROPE))
                e = extra(it, n - L_ROPE)
                if e and e[0] == "K":
                    rotate(*rope_x(hf, it, n - L_ROPE))
                if hf == 0 and live(it, n, 8, HEADS):
                    b, par = batch(0, it, n, 8), ((n - 8) // HEADS) % 2
                    pool.wait_ge(n_in[par], pair(0, it, n, 8) * 16)
                    gp.tensor_tensor(XN[:, par, 0, :], XN[:, par, 0, :], Bo[:, :], ALU.add)
                    gp.tensor_tensor(XN[:, par, 1, :], XN[:, par, 1, :], Bo[:, :], ALU.add).then_inc(n_sum, 1)
                if hf == 1:
                    tail(it, n)

            def tail(it, n):
                def at(lag):
                    return live(it, n, L_TAIL + lag, HEADS)

                def bp(lag):
                    return batch(0, it, n, L_TAIL + lag), ((n - L_TAIL - lag) // HEADS) % 2
                if at(0):
                    b, par = bp(0)
                    pool.wait_ge(x1_ve, b + 1)
                    gp.tensor_tensor(RS[:, par, :], VE[:, par, :], Mhalf[:, :], ALU.pow).then_inc(x1_rs, 1)
                if at(5):
                    b, _ = bp(5)
                    pool.wait_ge(mx_done, b + 1)
                    above(pool, qs_done, b)
                    gp.tensor_tensor(E2[:, :, :], KT[:, :, :], MX[:, :, 1:T + 1], ALU.subtract).then_inc(e2_arg, 1)
                if at(6):
                    b, _ = bp(6)
                    pool.wait_ge(e2_done, b + 1)
                    pool.wait_ge(v_in, 16 * b + 16)
                    above(pool, y_turned, TT * b)
                    gp.tensor_tensor(EV[:, :, :], E2[:, :, :], VT[:, :, :], ALU.mult).then_inc(e2v_done, 1)
                if at(7):
                    b, _ = bp(7)
                    pool.wait_ge(qs_done, b + 1)
                    pool.wait_ge(ad_done, b + 1)
                    gp.tensor_tensor(QS[:, :, 0:T], QS[:, :, 0:T], AD[:, :, :], ALU.mult).then_inc(aq_done, 1)
                if at(8):
                    b, _ = bp(8)
                    pool.wait_ge(ed_done, b + 1)
                    pool.wait_ge(ps_done, b + 1)
                    gp.tensor_tensor(EV[:, :, :], ED[:, :, :], VT[:, :, :], ALU.mult).then_inc(ev_done, 1)
                    pool.wait_ge(aq_done, b + 1)
                    gp.tensor_tensor(AD[:, :, :], PS[:, :, 0:T], AD[:, :, :], ALU.mult).then_inc(ap_done, 1)
                if at(9):
                    b, _ = bp(9)
                    pool.wait_ge(ap_done, b + 1)
                    gp.tensor_tensor(EV[:, :, :], EV[:, :, :], AD[:, :, :], ALU.add).then_inc(num_done, 1)
                if at(10):
                    b, _ = bp(10)
                    pool.wait_ge(num_done, b + 1)
                    pool.wait_ge(den_done, b + 1)
                    gp.tensor_tensor(EV[:, 0::2, :], EV[:, 0::2, :], A2[:, 1::2, :], ALU.mult)
                    gp.tensor_tensor(EV[:, 1::2, :], EV[:, 1::2, :], A2[:, 0::2, :], ALU.mult).then_inc(cross_done, 1)
                if at(L_Y + 2):
                    b, par = bp(L_Y + 2)
                    pool.wait_ge(x2_ve, b + 1)
                    gp.tensor_tensor(RS2[:, par, :], VE2[:, par, :], Mhalf[:, :], ALU.pow).then_inc(x2_rs, 1)

            pool.wait_ge(const_in, 16 * len(CONSTS))
            gp.tensor_scalar(NRb1, Rb1, -1.0, None, ALU.mult)
            gp.memset(Mhalf[:, :], -0.5)
            gp.memset(MX[:, :, 0:1], NEG)
            gp.memset(PS[:, :, 0:1], 0.0)
            gp.memset(QS[:, :, 0:1], 0.0).then_inc(consts, 1)
            pool.wait_ge(consts, 1)
            run_slots(pool, slot, (L_TAIL, L_TAIL + 17))

            def step(it, n):
                if stage_live(it, n, 1):
                    b, par = it * 2 + (n - 1), (n - 1) % 2
                    pool.wait_ge(f_turned, TT * b + TT)
                    above(pool, f_sum, TT * (b - 1))
                    for t in range(TT):
                        last = gp.tensor_tensor(X2B[par][:, t, :], XN[:, par, t, :], Fb[:, :], ALU.add)
                    last.then_inc(biased, 1)
                if stage_live(it, n, 3):
                    b, par = it * 2 + (n - 3), (n - 3) % 2
                    pool.wait_ge(f_ve, b + 1)
                    gp.tensor_tensor(RS[:, par, :], VE[:, par, :], Mhalf[:, :], ALU.pow).then_inc(f_rs, 1)

            pool.wait_ge(fb_in, 16)
            run_steps(pool, step, 3)

        @block.vector
        def _(dve):
            v = nc.vector

            def slot(hf, it, n):
                m = n % HEADS
                us = rotations(hf, it, n)
                for r, rp, _, dst, used in us:
                    dve.wait_ge(rotated, r + 1)
                    above(dve, rope_lo, r - 1)
                    v.tensor_tensor(RF[:, rp, :], RC[:, rp, :], RSN[:, rp, :], ALU.add).then_inc(summed, 1)
                s_live = live(it, n, L_S)
                if s_live:
                    g, i = head(hf, it, n, L_S), (n - L_S) % 2
                    dve.wait_ge(scored, g + 1)
                    above(dve, turned, g - 1)
                if live(it, n, L_OTL):
                    g, i = head(hf, it, n, L_OTL), (n - L_OTL) % SLOTS
                    j = (i % HEADS) // GROUP
                    dve.wait_ge(ot_hi, g + 1)
                    v.scalar_tensor_tensor(out=OT[1][:, i % 2, :], in0=ot_ps[:, 0:T], scalar=Bv[:, hf, j:j + 1],
                                           in1=OT[0][:, i % 2, :], op0=ALU.add, op1=ALU.subtract).then_inc(ot_lo, 1)
                if s_live:
                    g, i = head(hf, it, n, L_S), (n - L_S) % 2
                    for t, c in ((0, slice(0, P)), (1, slice(P, P + T))):
                        last = v.tensor_tensor_reduce(out=S[:, i, c], in0=s_ps[:, c], in1=Mask[:, c], scale=-SCALE,
                                                      scalar=3e38, op0=ALU.add, op1=ALU.min, accum_out=NM[:, i, t:t + 1])
                    last.then_inc(maxed, 1)
                if live(it, n, L_TAIL, HEADS):
                    b, par = batch(hf, it, n, L_TAIL), ((n - L_TAIL) // HEADS) % 2
                    dve.wait_ge(wo_done, HEADS * b + HEADS)
                    dve.wait_ge(n_in[par], pair(hf, it, n, L_TAIL) * 16)
                    if hf == 0:
                        dve.wait_ge(n_sum, b + 1)
                    above(dve, (r_out, x2_out)[hf][par], (pair(0, it, n, L_TAIL) - 1) * 16)
                    for t in range(TT):
                        last = v.tensor_tensor(RO[:, par, t, :], acc_ps[t][:, :], XN[:, par, t, :], ALU.add)
                    last.then_inc(acc_read, 1)
                for r, rp, _, dst, used in us:
                    dve.wait_ge(rope_hi, r + 1)
                    v.tensor_tensor(dst[1], RF[:, rp, :], dst[0], ALU.subtract).then_inc(rope_lo, 1)
                if hf == 1:
                    tail(it, n, 0)
                if live(it, n, L_PT):
                    g, i = head(hf, it, n, L_PT), (n - L_PT) % 2
                    dve.wait_ge(pt_hi, g + 1)
                    v.tensor_tensor(PT[1][:, i, :], pt_ps[:, 0:P + T], PT[0][:, i, :], ALU.subtract).then_inc(pt_lo, 1)
                if m == X_LO and more(it, n):
                    nb = it * 2 + (hf * BATCH + n // HEADS + 1)
                    dve.wait_ge(x_hi, nb + 1)
                    par = (n // HEADS + 1) % 2
                    v.tensor_tensor(X[1][:, par, :, :], XR[:, :, :], X[0][:, par, :, :], ALU.subtract).then_inc(x_lo, 1)
                if s_live:
                    g, i = head(hf, it, n, L_S), (n - L_S) % 2
                    dve.wait_ge(exped, g + 1)
                    v.reciprocal(RL[:, i, :], L[:, i, :]).then_inc(inverted, 1)
                e = extra(it, n)
                if e and e[0] == "V":
                    u, place, _ = unit_x(hf, it, n)
                    dve.wait_ge(evacuated, u + 1)
                    v.tensor_tensor(V[1][:, e[2], e[1], :], proj_ps[place][:, 0:T], V[0][:, e[2], e[1], :],
                                    ALU.subtract).then_inc(v_lo, 1)
                if hf == 1:
                    tail(it, n, 1)
                if hf == 1:
                    tail(it, n, 2)

            def norm_stats(par, ready, value, stats, mv, ve, done):
                dve.wait_ge(ready, value)
                for t in range(TT):
                    v.bn_stats(stats[:, par, t, :], RO[:, par, t, :])
                dve.drain()
                for t in range(TT):
                    v.bn_aggr(mv[:, par, t, :], stats[:, par, t, :])
                dve.drain()
                v.tensor_scalar(ve[:, par, :], mv[:, par, :, 1], EPS, None, ALU.add).then_inc(done, 1)

            def norm_apply(par, mv, rs, done):
                for t in range(TT):
                    last = v.tensor_scalar(RO[:, par, t, :], RO[:, par, t, :], mv[:, par, t, 0:1], rs[:, par, t:t + 1],
                                           ALU.subtract, ALU.mult)
                last.then_inc(done, 1)

            def tail(it, n, part):
                def at(lag, p):
                    return part == p and live(it, n, L_TAIL + lag, HEADS)

                def bp(lag):
                    return batch(0, it, n, L_TAIL + lag), ((n - L_TAIL - lag) // HEADS) % 2
                if at(0, 2):
                    b, par = bp(0)
                    norm_stats(par, acc_read, BATCH + b + 1, ST, MV, VE, x1_ve)
                if at(1, 1):
                    b, par = bp(1)
                    dve.wait_ge(x1_rs, b + 1)
                    norm_apply(par, MV, RS, x1_done)
                if at(4, 1):
                    b, _ = bp(4)
                    dve.wait_ge(kt_copied, TT * b + TT)
                    above(dve, e2_arg, b)
                    for c in range(KC):
                        last = v.tensor_tensor_scan(MX[:, c, 1:T + 1], Wb[:, c:c + 1].to_broadcast([P, T]), KT[:, c, :], NEG, ALU.add, ALU.max)
                    last.then_inc(mx_done, 1)
                if at(4, 2):
                    b, _ = bp(4)
                    dve.wait_ge(mx_done, b + 1)
                    for c in range(KC):
                        last = v.scalar_tensor_tensor(out=A2[:, c, :], in0=MX[:, c, 0:T], scalar=Wb[:, c:c + 1],
                                                      in1=MX[:, c, 1:T + 1], op0=ALU.add, op1=ALU.subtract)
                    last.then_inc(a2_arg, 1)
                if at(5, 0):
                    b, _ = bp(5)
                    for c in range(KC):
                        last = v.scalar_tensor_tensor(out=AD[:, c, :], in0=KT[:, c, :], scalar=Ub[:, c:c + 1],
                                                      in1=MX[:, c, 0:T], op0=ALU.add, op1=ALU.subtract)
                    last.then_inc(d_done, 1)
                if at(5, 1):
                    b, _ = bp(5)
                    dve.wait_ge(d_done, b + 1)
                    v.tensor_scalar(ED[:, :, :], AD[:, :, :], 0.0, None, ALU.min).then_inc(ed_arg, 1)
                if at(5, 2):
                    b, _ = bp(5)
                    v.tensor_scalar(AD[:, :, :], AD[:, :, :], 0.0, -1.0, ALU.max, ALU.mult).then_inc(ad_arg, 1)
                if at(6, 1):
                    b, _ = bp(6)
                    dve.wait_ge(a2_done, b + 1)
                    dve.wait_ge(e2_done, b + 1)
                    for c in range(KC):
                        last = v.tensor_tensor_scan(QS[:, c, 1:T + 1], A2[:, c, :], E2[:, c, :], 0.0, ALU.mult, ALU.add)
                    last.then_inc(qs_done, 1)
                if at(7, 0):
                    b, _ = bp(7)
                    dve.wait_ge(e2v_done, b + 1)
                    for c in range(KC):
                        last = v.tensor_tensor_scan(PS[:, c, 1:T + 1], A2[:, c, :], EV[:, c, :], 0.0, ALU.mult, ALU.add)
                    last.then_inc(ps_done, 1)
                if at(9, 0):
                    b, _ = bp(9)
                    dve.wait_ge(aq_done, b + 1)
                    dve.wait_ge(ed_done, b + 1)
                    dve.wait_ge(ps_done, b + 1)
                    v.tensor_tensor(A2[:, :, :], QS[:, :, 0:T], ED[:, :, :], ALU.add).then_inc(den_done, 1)
                if at(9, 1):
                    b, _ = bp(9)
                    dve.wait_ge(den_done, b + 1)
                    dve.wait_ge(ev_done, b + 1)
                    v.tensor_tensor(ED[:, 0:2, :], A2[:, 0::2, :], A2[:, 1::2, :], ALU.mult).then_inc(pairs_done, 1)
                if at(9, 2):
                    b, _ = bp(9)
                    dve.wait_ge(pairs_done, b + 1)
                    v.tensor_tensor(ED[:, 2, :], ED[:, 0, :], ED[:, 1, :], ALU.mult).then_inc(quad_done, 1)
                if at(10, 0):
                    b, _ = bp(10)
                    dve.wait_ge(quad_done, b + 1)
                    v.reciprocal(ED[:, 3, :], ED[:, 2, :]).then_inc(rquad_done, 1)
                if at(10, 2):
                    b, _ = bp(10)
                    dve.wait_ge(rquad_done, b + 1)
                    dve.wait_ge(num_done, b + 1)
                    v.tensor_tensor(AD[:, 0, :], ED[:, 3, :], ED[:, 1, :], ALU.mult)
                    v.tensor_tensor(AD[:, 1, :], ED[:, 3, :], ED[:, 0, :], ALU.mult).then_inc(rden_done, 1)
                if at(11, 2):
                    b, _ = bp(11)
                    dve.wait_ge(rden_done, b + 1)
                    dve.wait_ge(cross_done, b + 1)
                    for c in range(0, KC, 2):
                        last = v.tensor_tensor(EV[:, c:c + 2, :], EV[:, c:c + 2, :],
                                               AD[:, c // 2:c // 2 + 1, :].to_broadcast([P, 2, T]), ALU.mult)
                    last.then_inc(y_done, 1)
                for t in range(TT):
                    if at(L_Y + 1 + t, 0):
                        b, par = bp(L_Y + 1 + t)
                        dve.wait_ge(y_turned, TT * b + t + 1)
                        v.tensor_tensor(RO[:, par, t, :], tail_ps[:, :], RO[:, par, t, :], ALU.add).then_inc(x2_sum, 1)
                if at(L_Y + 2, 1):
                    b, par = bp(L_Y + 2)
                    norm_stats(par, x2_sum, TT * b + TT, ST2, MV2, VE2, x2_ve)
                if at(L_Y + 3, 0):
                    b, par = bp(L_Y + 3)
                    dve.wait_ge(x2_rs, b + 1)
                    norm_apply(par, MV2, RS2, x2_done)

            dve.wait_ge(const_in, 16 * len(CONSTS))
            dve.wait_ge(consts, 1)
            for hf in range(HALVES):
                for i in range(NP):
                    u = hf * NP + i
                    dve.wait_ge(w_hi, u + 1)
                    v.tensor_tensor(PIECES[hf][i][0][1], stage[:, u % 4, :], PIECES[hf][i][0][0], ALU.subtract).then_inc(w_lo, 1)
                    if i == TT + JL:
                        for n in range(FIRST, FIRST + X_LO + 1):
                            slot(hf, 0, n)
                peeled = PEELED[hf]
                for n in range(FIRST + X_LO + 1, peeled * SLOTS):
                    slot(hf, 0, n)
                with dve.Fori(peeled, TURNS - 1) as it:
                    for n in range(SLOTS):
                        slot(hf, it, n)
                for n in range(SLOTS + (L_TAIL + 1, L_TAIL + 17)[hf]):
                    slot(hf, TURNS - 1, n)

            def step(it, n):
                if stage_live(it, n, 3):
                    b = it * 2 + (n - 3)
                    dve.wait_ge(wt_hi, b + 1)
                    v.tensor_tensor(WT[1][:, :, :], bank[7][:, :].rearrange("p (r t) -> p r t", r=ER), WT[0][:, :, :], ALU.subtract).then_inc(wt_lo, 1)
                if stage_live(it, n, 2):
                    b, par = it * 2 + (n - 2), (n - 2) % 2
                    for t in range(TT):
                        dve.wait_ge(xt_hi, TT * b + (t + 1))
                        v.tensor_tensor(X[1][:, par, :, t * P:(t + 1) * P], bank[t][:, :].rearrange("p (c t) -> p c t", c=KC),
                                        X[0][:, par, :, t * P:(t + 1) * P], ALU.subtract).then_inc(xt_lo, 1)
                if stage_live(it, n, 2):
                    b = it * 2 + (n - 2)
                    dve.wait_ge(hid_exp, b + 1)
                    above(dve, logits_done, b)
                    v.tensor_scalar(HS, HE, 1.0, None, ALU.add).then_inc(hid_1p, 1)
                    dve.wait_ge(hid_1p, b + 1)
                    v.reciprocal(HS, HS).then_inc(hid_inv, 1)
                    dve.wait_ge(hid_inv, b + 1)
                    v.scalar_tensor_tensor(out=HS, in0=bank[2][0:HID, 0:T], scalar=Rb1, in1=HS, op0=ALU.add, op1=ALU.mult).then_inc(silu_done, 1)
                out_sum(it, n, 0)
                if stage_live(it, n, 2):
                    b = it * 2 + (n - 2)
                    dve.wait_ge(logits_done, b + 1)
                    lgp = bank[4][:, 0:TT * EXP].rearrange("p (a e) -> p a e", e=EXP)
                    for t in range(TT):
                        last = v.tensor_tensor(LG0[:, t, :], lgp[:, t, :], Rb2, ALU.add)
                    last.then_inc(lg_b, 1)
                    dve.wait_ge(lg_b, b + 1)
                    for t in range(TT):
                        last = v.tensor_tensor(LG[:, t, :], LG0[:, t, :], Gates, ALU.add)
                    last.then_inc(lg_g, 1)
                    dve.drain()
                    for t in range(TT):
                        v.max(M8[:, t, :], LG[:, t, :])
                    dve.drain()
                    v.tensor_tensor(DM, M8[:, :, 1:2], M8[:, :, 0:1], ALU.subtract).then_inc(top_diff, 1)
                    for t in range(TT):
                        v.max_index(IX[:, t, :], M8[:, t, :], LG[:, t, :])
                    dve.drain()
                    v.tensor_copy(I8, IX).then_inc(lg_sum, 1)
                    dve.wait_ge(top_exp, b + 1)
                    v.tensor_scalar(SE, EM, 1.0, None, ALU.add).then_inc(top_sum, 1)
                    dve.wait_ge(top_sum, b + 1)
                    v.reciprocal(P1, SE).then_inc(top_p1, 1)
                    dve.wait_ge(top_p1, b + 1)
                    v.tensor_tensor(P2, EM, P1, ALU.mult).then_inc(top_p2, 1)
                    dve.wait_ge(top_p2, b + 1)
                    dve.wait_ge(lg_sum, b + 1)
                    for t in range(TT):
                        v.tensor_scalar(C1[:, t, :], Iota, I8[:, t, 0:1], P1[:, t, :], ALU.is_equal, ALU.mult)
                        last = v.tensor_scalar(C2[:, t, :], Iota, I8[:, t, 1:2], P2[:, t, :], ALU.is_equal, ALU.mult)
                    last.then_inc(coef_parts, 1)
                    dve.wait_ge(coef_parts, b + 1)
                    v.tensor_tensor(CF, C1, C2, ALU.add).then_inc(coef_done, 1)
                    dve.wait_ge(coef_done, b + 1)
                    dve.wait_ge(low_done, b + 1)
                    above(dve, wt_turned, b)
                    for t in range(TT):
                        last = v.tensor_tensor(WX[:, t, :].rearrange("p (e r) -> p e r", e=EXP),
                                               bank[3][:, t * T:(t + 1) * T].rearrange("p (e r) -> p e r", e=EXP),
                                               CF[:, t, :].rearrange("p (e r) -> p e r", r=1).to_broadcast([P, EXP, RANK]), ALU.mult)
                    last.then_inc(weighted, 1)
                out_sum(it, n, 1)
                if stage_live(it, n, 3):
                    norm_stats((n - 3) % 2, f_sum, it * (2 * TT) + TT * (n - 2), ST, MV, VE, f_ve)
                if stage_live(it, n, 4):
                    b = it * 2 + (n - 4)
                    dve.wait_ge(f_rs, b + 1)
                    norm_apply(n % 2, MV, RS, f_done)

            def out_sum(it, n, t):
                if stage_live(it, n, 3):
                    b, par = it * 2 + (n - 3), (n - 3) % 2
                    dve.wait_ge(f_mm, TT * b + (t + 1))
                    if t == 0:
                        dve.wait_ge(biased, b + 1)
                        above(dve, f_out[par], (it + ((n - 3) // 2)) * 16)
                    v.tensor_tensor(RO[:, par, t, :], bank[5 + t][:, :], X2B[par][:, t, :], ALU.add).then_inc(f_sum, 1)

            for i, ((hi, lo), _) in enumerate(FFN):
                u = 2 * NP + i
                dve.wait_ge(w_hi, u + 1)
                v.tensor_tensor(lo, stage[:, u % 4, :], hi, ALU.subtract).then_inc(w_lo, 1)
            run_steps(dve, step, 4)


def layouts(i):
    g = lambda n: np.asarray(i[n])
    x, ctx = g("x"), g("ctx_2048")
    order = np.concatenate([np.arange(0, HD, 2), np.arange(1, HD, 2)])
    heads = np.array([[g_ * HKV + hf * JL + jl for jl in range(JL) for g_ in range(GROUP)] for hf in range(HALVES)])
    wq = g("L0_attn_Wq").reshape(KC, P, H, HD)[:, :, heads][..., order]
    wk = g("L0_attn_Wk").reshape(KC, P, HALVES, JL, HD)[..., order]
    wv = g("L0_attn_Wv").reshape(KC, P, HALVES, JL * HD)
    wo = g("L0_attn_Wo").reshape(H, HD, C)[heads]
    e = EXP
    row = lambda a: np.broadcast_to(a, (P, a.shape[0]))
    return dict(
        xt=x.reshape(BATCH, T, KC, P).transpose(0, 3, 2, 1), xn=x,
        ctxt=ctx.reshape(BATCH, T, KC, P).transpose(0, 3, 2, 1),
        wq=wq.transpose(2, 1, 3, 0, 4), wk=wk.transpose(2, 1, 3, 0, 4), wv=wv.transpose(2, 1, 0, 3),
        wo=wo.transpose(0, 2, 1, 3),
        bq=g("L0_attn_bq").reshape(H, HD)[heads][..., order].transpose(2, 0, 1),
        bk=g("L0_attn_bk").reshape(HALVES, JL, HD)[..., order].transpose(2, 0, 1),
        bv=g("L0_attn_bv").reshape(HALVES, JL, HD).transpose(2, 0, 1),
        bo=row(g("L0_attn_bo")),
        wdec=g("L0_xattn_w").reshape(KC, P).T, ubon=g("L0_xattn_u").reshape(KC, P).T,
        wf=g("L0_ffn_W").T.reshape(KC, P, C).transpose(1, 0, 2),
        wa=g("L0_ffn_A").reshape(EXP * RANK, KC, P).transpose(2, 1, 0),
        wb=g("L0_ffn_B").transpose(0, 2, 1).reshape(ER, P, C).transpose(1, 0, 2),
        rw1=np.concatenate([g("L0_ffn_rw1"), np.zeros((P - HID, C), x.dtype)]).reshape(P, KC, P).transpose(2, 1, 0),
        rw2=g("L0_ffn_rw2")[:e].T, fbias=row(g("L0_ffn_bias")), rb1=g("L0_ffn_rb1").reshape(HID, 1),
        rb2=row(g("L0_ffn_rb2")[:e]), gates=row(g("L0_ffn_gates")),
    )


def tables():
    theta = np.float32(1.0) / np.float32(10000.0) ** (np.arange(0, HD, 2, dtype=np.float32) / np.float32(HD))
    angle = (np.arange(T, dtype=np.float32)[None, :] * theta[:, None]).astype(np.float32)
    c, s = (f(angle.astype(np.float64)).astype(np.float32) for f in (np.cos, np.sin))
    tri = np.where(np.arange(P)[None, :] <= np.arange(P)[:, None], 0.0, MASKED).astype(np.float32)
    return dict(cos_t=np.concatenate([c, c]), sin_t=np.concatenate([-s, s]),
                mask_t=np.concatenate([tri, np.zeros((P, P), np.float32), tri], axis=1),
                ident_t=np.eye(P, dtype=np.float32),
                iota_t=np.broadcast_to(np.arange(EXP, dtype=np.float32), (P, EXP)))


def kernel(**inputs):
    import concourse.bacc as bacc
    from concourse.bass_utils import run_bass_kernel_spmd as run

    nc = bacc.Bacc("TRN2", target_bir_lowering=False, num_devices=1)
    arrays, args = {}, {}
    for name, a in (layouts(inputs) | tables()).items():
        arrays[f"in_{name}"] = a = np.ascontiguousarray(a)
        args[name] = nc.dram_tensor(f"in_{name}", a.shape, mybir.dt.from_np(a.dtype), kind="ExternalInput").ap()
    args["out"] = nc.dram_tensor("out_x", (BATCH, T, C), mybir.dt.float32, kind="ExternalOutput").ap()
    decoder(nc, **args)
    return run(nc, [arrays], core_ids=[0]).results[0]["out_x"]
```

```python
import numpy as np

import concourse.bass as bass
from concourse import mybir
from contextlib import ExitStack

BATCH, T, C = 16, 256, 512
H, HKV, HD = 16, 4, 128
P = 128
KC = C // P
TT = T // P
HALVES = 2
HEADS = H // HALVES
JL = HKV // HALVES
GROUP = H // HKV
SLOTS = 2 * HEADS
TURNS = BATCH // 2
ALL = BATCH * HEADS
EXP, RANK, HID = 16, 16, 64
ER = EXP * RANK // P
EPS = 1e-5
NEG = -1e38
MASKED = -3e38
SCALE = 1.0 / float(np.sqrt(H))

L_ROPE, L_SUM, L_S, L_T, L_PT, L_PV, L_WO = 1, 2, 3, 4, 5, 6, 7
L_OTL = L_WO
L_Y = 12
L_TAIL = HEADS - 1 + L_WO + 1
X_LO = 2
FIRST = -HEADS

WEIGHTS_AT = [-9, -8, -7, -6] + [h - 5 for h in range(HEADS)] + [h + 3 for h in range(HEADS)]
FFN_WEIGHTS_AT = SLOTS + 1
STEPS_AT = [24, 26, 28, 30, 32]
LAST_SLOT = HEADS + L_TAIL + 16

PEELED = (2, 3, 3)

UNITS = HEADS + TT + JL
Q_UNIT = [0, 1, 2, 3, 4, 6, 8, 10]
X_UNIT = {4: 5, 5: 7, 6: 9, 7: 11}
ROPES = HEADS + JL
Q_ROPE = [0, 1, 2, 3, 4, 6, 8, 9]
X_ROPE = {4: 5, 5: 7}


def decoder(nc, xt, xn, ctxt, wq, wk, wv, wo, bq, bk, bv, bo, wdec, ubon, wf, wa, wb, rw1, rw2,
            fbias, rb1, rb2, gates, cos_t, sin_t, mask_t, ident_t, iota_t, out):
    fp32, fr, u32 = mybir.dt.float32, mybir.dt.float32r, mybir.dt.uint32
    ALU, ACT = mybir.AluOpType, mybir.ActivationFunctionType

    ctx = ExitStack()
    with ctx:
        def sb(name, shape, dt=fp32):
            return ctx.enter_context(nc.sbuf_tensor(name, shape, dt))

        def sem(name):
            return ctx.enter_context(nc.semaphore(name))

        resid = nc.dram_tensor("resid", (BATCH, T, C), fp32, kind="Internal").ap()
        mixed = nc.dram_tensor("mixed", (BATCH, T, C), fp32, kind="Internal").ap()

        Wq = [sb(f"Wq{i}", [P, HEADS, KC, HD], fr) for i in "hl"]
        Wk = [sb(f"Wk{i}", [P, JL, KC, HD], fr) for i in "hl"]
        Wv = [sb(f"Wv{i}", [P, KC, JL * HD], fr) for i in "hl"]
        Wo = [sb(f"Wo{i}", [P, HEADS, C], fr) for i in "hl"]
        Bq = sb("Bq", [P, HALVES, HEADS])
        Bk = sb("Bk", [P, HALVES, JL])
        Bv = sb("Bv", [P, HALVES, JL])
        Cos = sb("Cos", [P, T])
        Sin = sb("Sin", [P, T])
        Mask = sb("Mask", [P, P + T])
        Ident = sb("Ident", [P, P])
        Wb = sb("Wb", [P, KC])
        Ub = sb("Ub", [P, KC])
        Bo = sb("Bo", [P, C])
        XR = sb("XR", [P, KC, T])
        ffn_stage = lambda i: XR[:, i % 2 * 2:i % 2 * 2 + 2, :].rearrange("p k t -> p (k t)")
        X = [sb(f"X{i}", [P, 2, KC, T], fr) for i in "hl"]
        K = [sb(f"K{i}", [P, 2, JL, T], fr) for i in "hl"]
        V = [sb(f"V{i}", [P, 2, TT, JL * HD], fr) for i in "hl"]
        QB = sb("QB", [P, 2, T])
        SW = sb("SW", [P, 2, T])
        RC = sb("RC", [P, 2, T])
        RSN = sb("RSN", [P, 2, T])
        RF = sb("RF", [P, 2, T])
        Q = [sb(f"Q{i}", [P, 2, T], fr) for i in "hl"]
        S = sb("S", [P, 2, P + T])
        NM = sb("NM", [P, 2, TT])
        L = sb("L", [P, 2, TT])
        RL = sb("RL", [P, 2, TT])
        PT = [sb(f"PT{i}", [P, 2, P + T], fr) for i in "hl"]
        OT = [sb(f"OT{i}", [P, 2, T], fr) for i in "hl"]
        XN = sb("XN", [P, 2, TT, C])
        RO = sb("RO", [P, 2, TT, C])
        KVT = sb("KVT", [P, 2, KC, T])
        KT, VT = KVT[:, 0, :, :], KVT[:, 1, :, :]
        stage = KVT[:, :, :, :].rearrange("p a k t -> p (a k t)").rearrange("p (s n) -> p s n", s=4)
        MX = sb("MX", [P, KC, T + 1])
        PS = sb("PS", [P, KC, T + 1])
        QS = sb("QS", [P, KC, T + 1])
        A2 = sb("A2", [P, KC, T])
        E2 = sb("E2", [P, KC, T])
        AD = sb("AD", [P, KC, T])
        ED = sb("ED", [P, KC, T])
        EV = sb("EV", [P, KC, T])
        ST = sb("ST", [P, 2, TT, 6])
        MV = sb("MV", [P, 2, TT, 2])
        VE = sb("VE", [P, 2, TT])
        RS = sb("RS", [P, 2, TT])
        ST2 = sb("ST2", [P, 2, TT, 6])
        MV2 = sb("MV2", [P, 2, TT, 2])
        VE2 = sb("VE2", [P, 2, TT])
        RS2 = sb("RS2", [P, 2, TT])
        Mhalf = sb("Mhalf", [P, TT])

        wq_flat = [w[:, :, :, :].rearrange("p h k n -> p (h k n)") for w in Wq]
        Wf = [w[:, 0:KC * C].rearrange("p (k n) -> p k n", k=KC) for w in wq_flat]
        Wa = [w[:, KC * C:KC * C + KC * EXP * RANK].rearrange("p (k n) -> p k n", k=KC) for w in wq_flat]
        Wd = [w[:, 3072:4096].rearrange("p (k n) -> p k n", k=ER) for w in wq_flat]
        Wr = [w[:, 0, :, :] for w in Wk]
        flat = lambda a: a[:, :, :].rearrange("p a t -> p (a t)")
        X2B = [[flat(SW), flat(RSN)], [flat(RF), flat(S)[:, 256:256 + C]]]
        OUT = [RO[:, 0, :, :], XR[:, :, :].rearrange("p k t -> p (k t)").rearrange("p (a c) -> p a c", a=TT)]
        WX = QB[:, :, :]
        WT = [a[:, :, :] for a in Q]
        HE, HS = RC[0:HID, 0, :], RC[0:HID, 1, :]
        Fb = Bo
        small = sb("small", [P, 96])
        Rw2, Rb1, NRb1 = small[0:HID, 0:16], small[0:HID, 16:17], small[0:HID, 17:18]
        Rb2, Gates, Iota = small[:, 32:48], small[:, 48:64], small[:, 64:80]
        s_flat = S[:, :, :].rearrange("p a n -> p (a n)")
        cut = lambda at, n, k: s_flat[:, at:at + n].rearrange("p (a k) -> p a k", k=k)
        LG0, LG1, LG = cut(0, 32, EXP), cut(32, 32, EXP), cut(64, 32, EXP)
        M8, I8 = cut(96, 16, 8), cut(112, 16, 8)
        IX = cut(128, 16, 8).bitcast(u32)
        DM, EM, SE, P1, P2 = (cut(144 + 2 * k, 2, 1) for k in range(5))
        C1, C2, CF = cut(160, 32, EXP), cut(192, 32, EXP), cut(224, 32, EXP)

        bank = [ctx.enter_context(nc.psum_tensor(f"bank{i}", [P, 512], fp32)) for i in range(8)]
        proj_ps = bank[0:2]
        s_ps, pt_ps, ot_ps, tail_ps = bank[2], bank[3], bank[4], bank[7]
        acc_ps = bank[5:7]

        const_in = sem("const_in")
        stage_in = [sem(f"stage_in{i}") for i in range(4)]
        f_stage_in = [sem(f"f_stage_in{i}") for i in range(2)]
        w_hi, w_lo = sem("w_hi"), sem("w_lo")
        consts = sem("consts")
        x_in, x_hi, x_lo = sem("x_in"), sem("x_hi"), sem("x_lo")
        n_in, r_out = ([sem(f"{n}{i}") for i in range(2)] for n in ("n_in", "r_out"))
        n_sum = sem("n_sum")
        projected, evacuated, v_lo = sem("projected"), sem("evacuated"), sem("v_lo")
        swapped = [sem(f"swapped{i}") for i in range(2)]
        rotated, summed = sem("rotated"), sem("summed")
        rope_hi, rope_lo = sem("rope_hi"), sem("rope_lo")
        scored, maxed, exped, inverted, normed = (sem(n) for n in ("scored", "maxed", "exped", "inverted", "normed"))
        turned, pt_hi, pt_lo = sem("turned"), sem("pt_hi"), sem("pt_lo")
        mixed_v, ot_hi, ot_lo, wo_done = sem("mixed_v"), sem("ot_hi"), sem("ot_lo"), sem("wo_done")
        acc_read = sem("acc_read")
        x1_ve, x1_rs, x1_done = sem("x1_ve"), sem("x1_rs"), sem("x1_done")
        x1_turned, kt_copied = sem("x1_turned"), sem("kt_copied")
        v_in = sem("v_in")
        mx_done, a2_arg, e2_arg, a2_done, e2_done = (sem(n) for n in ("mx_done", "a2_arg", "e2_arg", "a2_done", "e2_done"))
        d_done, ed_arg, ad_arg, ad_done, ed_done = (sem(n) for n in ("d_done", "ed_arg", "ad_arg", "ad_done", "ed_done"))
        e2v_done, ev_done, qs_done, ps_done = sem("e2v_done"), sem("ev_done"), sem("qs_done"), sem("ps_done")
        aq_done, den_done, pairs_done, quad_done = (sem(n) for n in ("aq_done", "den_done", "pairs_done", "quad_done"))
        rquad_done, rden_done, cross_done = sem("rquad_done"), sem("rden_done"), sem("cross_done")
        ap_done, num_done, y_done = sem("ap_done"), sem("num_done"), sem("y_done")
        y_turned, x2_sum, x2_ve, x2_rs, x2_done = (sem(n) for n in ("y_turned", "x2_sum", "x2_ve", "x2_rs", "x2_done"))
        x2_out = [sem(f"x2_out{i}") for i in range(2)]

        f_in = [sem(f"f_in{i}") for i in range(2)]
        f_const, fb_in = sem("f_const"), sem("fb_in")
        f_turned, xt_hi, xt_lo, biased, f_ready = (sem(n) for n in ("f_turned", "xt_hi", "xt_lo", "biased", "f_ready"))
        hid_done, hid_exp, hid_1p, hid_inv, silu_done = (sem(n) for n in ("hid_done", "hid_exp", "hid_1p", "hid_inv", "silu_done"))
        low_done, logits_done, lg_b, lg_g, lg_sum = (sem(n) for n in ("low_done", "logits_done", "lg_b", "lg_g", "lg_sum"))
        top_diff, top_exp, top_sum, top_p1, top_p2 = (sem(n) for n in ("top_diff", "top_exp", "top_sum", "top_p1", "top_p2"))
        coef_parts, coef_done, weighted = sem("coef_parts"), sem("coef_done"), sem("weighted")
        wt_turned, wt_hi, wt_lo, f_mm, f_sum = (sem(n) for n in ("wt_turned", "wt_hi", "wt_lo", "f_mm", "f_sum"))
        f_ve, f_rs, f_done = sem("f_ve"), sem("f_rs"), sem("f_done")
        f_out = [sem(f"f_out{i}") for i in range(2)]

        def live(hf, it, n, lag, step=1):
            if (n - lag) % step:
                return False
            return not isinstance(it, int) or -ALL * hf <= it * SLOTS + n - lag < ALL

        def tail_live(it, n, lag):
            if (n - L_TAIL - lag) % HEADS:
                return False
            return not isinstance(it, int) or 0 <= it * SLOTS + n - L_TAIL - lag < ALL

        def pass_of(hf, it, n, lag):
            return 0 if isinstance(it, int) and it * SLOTS + n < lag else hf

        def head(hf, it, n, lag):
            return it * SLOTS + (hf * ALL + n - lag)

        def batch(hf, it, n, lag):
            return it * 2 + (hf * BATCH + (n - lag) // HEADS)

        def pair(hf, it, n, lag):
            return it + ((hf * BATCH + (n - lag) // HEADS) // 2 + 1)

        def numbered(hf, it, k, per, before, q_order, x_order):
            m, q = k % HEADS, q_order is not None
            if hf == 0 and isinstance(it, int) and it * SLOTS + k < 0:
                at = sorted(x_order).index(m)
                return at, at % 2, at // 2 + 1
            last = hf == 1 and isinstance(it, int) and it * 2 + k // HEADS == BATCH - 1
            at = (m if last else q_order[m]) if q else x_order[m]
            at += (hf * BATCH + k // HEADS) * per + before
            return it * (2 * per) + at, at % 2, it * per + (at // 2 + 1)

        def unit_q(hf, it, k):
            return numbered(hf, it, k, UNITS, TT + JL, Q_UNIT, None)

        def unit_x(hf, it, k):
            return numbered(hf, it, k, UNITS, TT + JL, None, X_UNIT)

        def rope_q(hf, it, k):
            return numbered(hf, it, k, ROPES, JL, Q_ROPE, None)

        def rope_x(hf, it, k):
            return numbered(hf, it, k, ROPES, JL, None, X_ROPE)

        def above(eng, s, value):
            assert isinstance(value, int) or value.min_val > 0
            if not isinstance(value, int) or value > 0:
                eng.wait_ge(s, value)

        def more(hf, it, n):
            return hf == 0 or not isinstance(it, int) or it * 2 + n // HEADS + 1 < BATCH

        def next_batch(hf, it, n):
            if isinstance(it, int):
                b = hf * BATCH + it * 2 + n // HEADS + 1
                return b // BATCH, b % BATCH
            return hf, it * 2 + (n // HEADS + 1)

        def extra(hf, it, n):
            m = n % HEADS
            if m < 4 or not more(hf, it, n):
                return None
            par = (n // HEADS + 1) % 2
            return ("K", m - 4, par) if m < 6 else ("V", m - 6, par)

        def run_slots(eng, slot, weights=None, ffn_weights=None, step=None, ahead=0):
            def go(hf, it, n):
                slot(hf, it, n)
                if weights and isinstance(it, int):
                    for p in range(hf, HALVES):
                        for i in range(NP):
                            if WEIGHTS_AT[i] - ahead == it * SLOTS + n + (hf - p) * ALL:
                                weights(p, i)

            if weights:
                for i in range(NP):
                    if WEIGHTS_AT[i] - ahead < FIRST:
                        weights(0, i)
            for n in range(FIRST, PEELED[0] * SLOTS):
                go(0, 0, n)
            with eng.Fori(PEELED[0], TURNS - 1) as it:
                for n in range(SLOTS):
                    go(0, it, n)
            for n in range(SLOTS):
                go(0, TURNS - 1, n)
            for n in range(PEELED[1] * SLOTS):
                go(1, 0, n)
            with eng.Fori(PEELED[1], TURNS - 1) as it:
                for n in range(SLOTS):
                    go(1, it, n)
            for n in range(LAST_SLOT + 1):
                go(1, TURNS - 1, n)
                if ffn_weights and 0 <= n + ahead - FFN_WEIGHTS_AT < len(FFN):
                    ffn_weights(n + ahead - FFN_WEIGHTS_AT)
                if n in STEPS_AT:
                    step(0, STEPS_AT.index(n))

        def pieces(hf):
            for j in range(JL):
                yield [w[:, j, :, :].rearrange("p k n -> p (k n)") for w in Wk], wk[hf, :, j, :, :].rearrange("p k n -> p (k n)")
            for kc in range(0, KC, 2):
                yield [w[:, kc:kc + 2, :].rearrange("p k n -> p (k n)") for w in Wv], wv[hf, :, kc:kc + 2, :].rearrange("p k n -> p (k n)")
            for h in range(HEADS):
                yield [w[:, h, :, :].rearrange("p k n -> p (k n)") for w in Wq], wq[hf, :, h, :, :].rearrange("p k n -> p (k n)")
            for h in range(HEADS):
                yield [w[:, h, :] for w in Wo], wo[hf, :, h, :]
        def ffn_pieces():
            yield [w.rearrange("p k n -> p (k n)") for w in Wr], rw1.rearrange("p k n -> p (k n)")
            for k in range(0, KC, 2):
                yield [w[:, k:k + 2, :].rearrange("p k n -> p (k n)") for w in Wa], wa[:, k:k + 2, :].rearrange("p k n -> p (k n)")
            for k in range(KC):
                yield [w[:, k, :] for w in Wf], wf[:, k, :]
            for k in range(ER):
                yield [w[:, k, :] for w in Wd], wb[:, k, :]

        def run_steps(eng, step, trailing):
            for n in range(len(STEPS_AT), 2 * PEELED[2]):
                step(0, n)
            with eng.Fori(PEELED[2], TURNS) as it:
                for n in range(2):
                    step(it, n)
            for n in range(trailing):
                step(TURNS, n)

        def stage_live(it, n, lag):
            return not isinstance(it, int) or 0 <= it * 2 + n - lag < BATCH

        PIECES = [list(pieces(hf)) for hf in range(HALVES)]
        NP = len(PIECES[0])
        FFN = list(ffn_pieces())
        CONSTS = [(Bq, bq), (Bk, bk), (Bv, bv), (Cos, cos_t), (Sin, sin_t), (Mask, mask_t),
                  (Ident, ident_t), (Wb, wdec), (Ub, ubon), (Bo, bo), (Iota, iota_t),
                  (Rb2, rb2), (Gates, gates), (Rw2, rw2), (Rb1, rb1)]

        def rotations(hf, it, n):
            found = []
            k = n - L_SUM
            if live(hf, it, n, L_SUM):
                found.append((*rope_q(hf, it, k), [a[:, k % 2, :] for a in Q], head(hf, it, k, 0) - 1))
            e = extra(hf, it, k)
            if e and e[0] == "K":
                found.append((*rope_x(hf, it, k), [a[:, e[2], e[1], :] for a in K],
                              it * SLOTS + (hf * ALL + k // HEADS * HEADS)))
            return found

        block = ctx.enter_context(nc.Block())

        @block.sync
        def _(sp):
            def slot(hf, it, n):
                m = n % HEADS
                if m == 0 and more(hf, it, n):
                    p, b = next_batch(hf, it, n)
                    above(sp, x_lo, b + p * BATCH)
                    sp.dma_start(XR[:, :, :], xt[b, :, :, :]).then_inc(x_in, 16)
                if live(hf, it, n, 0):
                    r = rope_q(hf, it, n)[1]
                    sp.wait_ge(evacuated, unit_q(hf, it, n)[0] + 1)
                    sp.dma_start(SW[0:64, r, :], QB[64:128, r, :]).then_inc(swapped[r], 16)
                    sp.dma_start(SW[64:128, r, :], QB[0:64, r, :]).then_inc(swapped[r], 16)
                e = extra(hf, it, n)
                if e and e[0] == "K":
                    r = rope_x(hf, it, n)[1]
                    sp.wait_ge(evacuated, unit_x(hf, it, n)[0] + 1)
                    sp.dma_start(SW[0:64, r, :], QB[64:128, r, :]).then_inc(swapped[r], 16)
                    sp.dma_start(SW[64:128, r, :], QB[0:64, r, :]).then_inc(swapped[r], 16)
                if live(hf, it, n, 4, HEADS):
                    par = ((n - 4) // HEADS) % 2
                    b = batch(0, it, n, 4)
                    above(sp, acc_read, batch(hf, it, n, 4) - 1)
                    if hf == 1 and isinstance(it, int) and it == 0 and b < 2:
                        sp.wait_ge(r_out[par], 16 * BATCH // 2)
                    sp.dma_start(XN[:, par, :, :], (xn if hf == 0 else resid)[b, :, :].rearrange("(a p) c -> p a c", p=P)).then_inc(n_in[par], 16)
                if live(hf, it, n, L_TAIL + 1, HEADS) and pass_of(hf, it, n, L_TAIL + 1) == 0:
                    par = ((n - L_TAIL - 1) // HEADS) % 2
                    b = batch(hf, it, n, L_TAIL + 1)
                    sp.wait_ge(acc_read, b + 1)
                    sp.dma_start(resid[b, :, :].rearrange("(a p) c -> p a c", p=P), RO[:, par, :, :]).then_inc(r_out[par], 16)
                if hf == 1 and tail_live(it, n, 2):
                    b = batch(0, it, n, L_TAIL + 2)
                    above(sp, ev_done, b)
                    if isinstance(it, int) and it == 0 and n < SLOTS + L_TAIL:
                        sp.wait_ge(w_lo, HALVES * NP)
                    sp.dma_start(VT[:, :, :], ctxt[b, :, :, :]).then_inc(v_in, 16)
                if hf == 1 and tail_live(it, n, 15):
                    par = ((n - L_TAIL - 14) // HEADS) % 2
                    b = batch(0, it, n, L_TAIL + 15)
                    sp.wait_ge(x2_done, b + 1)
                    sp.dma_start(mixed[b, :, :].rearrange("(a p) c -> p a c", p=P), RO[:, par, :, :]).then_inc(x2_out[par], 16)

            def step(it, n):
                if stage_live(it, n, 0):
                    b = it * 2 + n
                    above(sp, biased, b - 1)
                    if isinstance(it, int) and n < 2:
                        sp.wait_ge(acc_read, HALVES * BATCH)
                    if isinstance(it, int):
                        sp.wait_ge(x2_out[n % 2], 16 * (BATCH // 2 - (n < len(STEPS_AT))))
                    sp.dma_start(XN[:, n % 2, :, :], mixed[b, :, :].rearrange("(a p) c -> p a c", p=P)).then_inc(f_in[n % 2], 16)
                if stage_live(it, n, 4):
                    b = it * 2 + (n - 4)
                    sp.wait_ge(f_done, b + 1)
                    sp.dma_start(out[b, :, :].rearrange("(a p) c -> p a c", p=P), OUT[n % 2]).then_inc(f_out[n % 2], 16)

            def weights(hf, i):
                u = hf * NP + i
                if u >= 4:
                    sp.wait_ge(w_lo, u - 3)
                sp.dma_start(stage[:, u % 4, :], PIECES[hf][i][1]).then_inc(stage_in[u % 4], 16)
                if u == 3:
                    for dst, src in CONSTS:
                        sp.dma_start(dst[tuple(slice(None) for _ in dst.shape)], src).then_inc(const_in, 16)

            def ffn_weights(i):
                if i == 0:
                    sp.wait_ge(x_lo, HALVES * BATCH)
                    sp.wait_ge(acc_read, BATCH)
                    sp.dma_start(Fb[:, :], fbias).then_inc(fb_in, 16)
                if i >= 2:
                    sp.wait_ge(w_lo, HALVES * NP + i - 1)
                sp.dma_start(ffn_stage(i), FFN[i][1]).then_inc(f_stage_in[i % 2], 16)

            run_slots(sp, slot, weights, ffn_weights, step, ahead=2)
            run_steps(sp, step, 4)
            for i in range(2):
                sp.wait_ge(f_out[i], 16 * BATCH // 2)
        @block.tensor
        def _(pe):
            def three(dst, lhs, rhs, first=True, last=True):
                nc.tensor.matmul(dst, lhs[0], rhs[0], start=first, stop=False)
                nc.tensor.matmul(dst, lhs[0], rhs[1], start=False, stop=False)
                return nc.tensor.matmul(dst, lhs[1], rhs[0], start=False, stop=last)

            def slot(hf, it, n):
                m = n % HEADS
                if live(hf, it, n, L_S):
                    g, i = head(hf, it, n, L_S), (n - L_S) % SLOTS
                    par, j, q = i // HEADS, (i % HEADS) // GROUP, i % 2
                    pe.wait_ge(rope_lo, rope_q(hf, it, n - L_S)[0] + 1)
                    above(pe, maxed, g)
                    for t, c0, keys in ((0, 0, P), (1, P, T)):
                        last = three(s_ps[:, c0:c0 + keys], [a[:, q, t * P:(t + 1) * P] for a in Q],
                                     [a[:, par, j, 0:keys] for a in K])
                    last.then_inc(scored, 1)
                if live(hf, it, n, 0):
                    u, place, _ = unit_q(hf, it, n)
                    par = (n // HEADS) % 2
                    if isinstance(it, int) and it == 0 and n < HEADS:
                        pe.wait_ge(w_lo, hf * NP + JL + TT + m + 1)
                    if m == 1:
                        pe.wait_ge(v_lo, it * (2 * TT) + (hf * BATCH + n // HEADS + 1) * TT)
                    above(pe, evacuated, u - 1)
                    dst = proj_ps[place][:, 0:T]
                    for kc in range(KC):
                        last = three(dst, [w[:, m, kc, :] for w in Wq], [x[:, par, kc, :] for x in X],
                                     kc == 0, kc == KC - 1)
                    last.then_inc(projected, 1)
                if live(hf, it, n, L_PV):
                    g, i = head(hf, it, n, L_PV), (n - L_PV) % SLOTS
                    par, j = i // HEADS, (i % HEADS) // GROUP
                    pe.wait_ge(pt_lo, g + 1)
                    if i % HEADS == 0:
                        pe.wait_ge(v_lo, (batch(hf, it, n, L_PV) + 1) * TT)
                    above(pe, ot_lo, g)
                    vs = [[v[:, par, t, j * HD:(j + 1) * HD] for v in V] for t in range(TT)]
                    three(ot_ps[:, 0:T], vs[0], [a[:, i % 2, 0:T] for a in PT], True, False)
                    three(ot_ps[:, P:T], vs[1], [a[:, i % 2, T:T + P] for a in PT], False, True).then_inc(mixed_v, 1)
                e = extra(hf, it, n)
                if e:
                    kind, tile, par = e
                    u, place, _ = unit_x(hf, it, n)
                    dst = proj_ps[place][:, 0:T]
                    nb = it * 2 + (hf * BATCH + n // HEADS + 1)
                    if m == 4:
                        pe.wait_ge(x_lo, nb + 1)
                    if isinstance(nb, int) and nb % BATCH == 0:
                        pe.wait_ge(w_lo, next_batch(hf, it, n)[0] * NP + (tile + 1 if kind == "K" else JL + TT))
                    if m == 7:
                        pe.wait_ge(v_lo, nb * TT + 1)
                    above(pe, evacuated, u - 1)
                    for kc in range(KC):
                        if kind == "V":
                            last = three(dst, [x[:, par, kc, tile * P:(tile + 1) * P] for x in X],
                                         [w[:, kc, :] for w in Wv], kc == 0, kc == KC - 1)
                        else:
                            last = three(dst, [w[:, tile, kc, :] for w in Wk],
                                         [x[:, par, kc, :] for x in X], kc == 0, kc == KC - 1)
                    last.then_inc(projected, 1)
                if live(hf, it, n, L_WO):
                    g, i = head(hf, it, n, L_WO), (n - L_WO) % SLOTS
                    h = i % HEADS
                    pe.wait_ge(ot_lo, g + 1)
                    if isinstance(it, int) and it == 0 and 0 <= n - L_WO < HEADS:
                        pe.wait_ge(w_lo, hf * NP + JL + TT + HEADS + h + 1)
                    if h == 0:
                        above(pe, acc_read, batch(hf, it, n, L_WO))
                    for t in range(TT):
                        last = three(acc_ps[t][:, :], [a[:, i % 2, t * P:(t + 1) * P] for a in OT],
                                     [w[:, h, :] for w in Wo], h == 0, h == HEADS - 1)
                    last.then_inc(wo_done, 1)
                if hf == 1:
                    for t in range(TT):
                        if tail_live(it, n, 2 + t):
                            turn_x1(hf, it, n, t)
                        if tail_live(it, n, L_Y + t):
                            turn_y(hf, it, n, t)
                if live(hf, it, n, L_T):
                    g, i = head(hf, it, n, L_T), (n - L_T) % SLOTS
                    pe.wait_ge(normed, g + 1)
                    above(pe, pt_lo, g)
                    if isinstance(it, int) and g == 0:
                        pe.wait_ge(const_in, 16 * len(CONSTS))
                    for k in range(3):
                        last = nc.tensor.transpose(pt_ps[:, k * P:(k + 1) * P], S[:, i % 2, k * P:(k + 1) * P], Ident[:, :])
                    last.then_inc(turned, 1)

            def turn_x1(hf, it, n, t):
                b = batch(0, it, n, L_TAIL + 2 + t)
                par = ((n - L_TAIL - 2 - t) // HEADS) % 2
                pe.wait_ge(x1_done, b + 1)
                if t == 0:
                    above(pe, x2_sum, TT * (b - 1))
                else:
                    pe.wait_ge(kt_copied, TT * b + t)
                for c in range(KC):
                    last = nc.tensor.transpose(tail_ps[:, c * P:(c + 1) * P], RO[:, par, t, c * P:(c + 1) * P], Ident[:, :])
                last.then_inc(x1_turned, 1)

            def turn_y(hf, it, n, t):
                b = batch(0, it, n, L_TAIL + L_Y + t)
                pe.wait_ge(y_done, b + 1)
                if t == 0:
                    if isinstance(it, int) and b == BATCH - 1 and len(STEPS_AT) > 3:
                        pe.wait_ge(wt_lo, len(STEPS_AT) - 3)
                    if isinstance(it, int):
                        pe.wait_ge(kt_copied, TT * min(b + 2, BATCH))
                    else:
                        pe.wait_ge(kt_copied, TT * b + 2 * TT)
                else:
                    pe.wait_ge(x2_sum, TT * b + t)
                for c in range(KC):
                    last = nc.tensor.transpose(tail_ps[:, c * P:(c + 1) * P], EV[:, c, t * P:(t + 1) * P], Ident[:, :])
                last.then_inc(y_turned, 1)

            def step(it, n):
                def low_rank(t):
                    if stage_live(it, n, 2):
                        par = n % 2
                        b = it * 2 + (n - 2)
                        if t == 0:
                            above(pe, weighted, b - 1)
                        else:
                            pe.wait_ge(xt_lo, TT * b + TT)
                        for k in range(KC):
                            last = three(bank[3 + par][:, t * T:(t + 1) * T], [x[:, par, k, t * P:(t + 1) * P] for x in X],
                                         [w[:, k, :] for w in Wa], k == 0, k == KC - 1)
                        last.then_inc(low_done, 1)

                def turn_x2(t):
                    if stage_live(it, n, 1):
                        b, par = it * 2 + (n - 1), (n - 1) % 2
                        if t == 0:
                            pe.wait_ge(f_in[par], (it + ((n - 1) // 2 + 1)) * 16)
                        above(pe, xt_lo, TT * (b - 1) + (t + 1))
                        for c in range(KC):
                            last = nc.tensor.transpose(bank[t][:, c * P:(c + 1) * P], XN[:, par, t, c * P:(c + 1) * P], Ident[:, :])
                        last.then_inc(f_turned, 1)

                def dense(t):
                    if stage_live(it, n, 3):
                        b, par = it * 2 + (n - 3), (n - 3) % 2
                        above(pe, f_sum, TT * (b - 1) + (t + 1))
                        for k in range(KC):
                            three(bank[5 + t][:, :], [x[:, par, k, t * P:(t + 1) * P] for x in X], [w[:, k, :] for w in Wf], k == 0, False)

                def delta(t):
                    if stage_live(it, n, 3):
                        b = it * 2 + (n - 3)
                        if t == 0:
                            pe.wait_ge(wt_lo, b + 1)
                        for r in range(ER):
                            last = three(bank[5 + t][:, :], [a[:, r, t * P:(t + 1) * P] for a in WT], [w[:, r, :] for w in Wd], False, r == ER - 1)
                        last.then_inc(f_mm, 1)

                if stage_live(it, n, 2):
                    b, par = it * 2 + (n - 2), n % 2
                    if isinstance(it, int) and b == 0:
                        pe.wait_ge(w_lo, HALVES * NP + len(FFN))
                    pe.wait_ge(xt_lo, TT * b + 1)
                low_rank(0)
                if stage_live(it, n, 2):
                    pe.wait_ge(xt_lo, TT * b + TT)
                    above(pe, silu_done, b)
                    for k in range(KC):
                        last = three(bank[2][:, 0:T], [w[:, k, :] for w in Wr], [x[:, par, k, :] for x in X], k == 0, k == KC - 1)
                    last.then_inc(hid_done, 1)
                low_rank(1)
                if stage_live(it, n, 3):
                    b = it * 2 + (n - 3)
                    pe.wait_ge(weighted, b + 1)
                    above(pe, wt_lo, b)
                    if isinstance(it, int):
                        pe.wait_ge(kt_copied, TT * BATCH)
                        pe.wait_ge(x2_sum, TT * (BATCH - (n < len(STEPS_AT))))
                    for r in range(ER):
                        for t in range(TT):
                            last = nc.tensor.transpose(bank[7][:, r * T + t * P:r * T + (t + 1) * P], WX[:, t, r * P:(r + 1) * P], Ident[:, :])
                    last.then_inc(wt_turned, 1)
                dense(0)
                if stage_live(it, n, 2):
                    b = it * 2 + (n - 2)
                    pe.wait_ge(silu_done, b + 1)
                    above(pe, lg_b, b)
                    for a in range(TT):
                        last = nc.tensor.matmul(bank[2][:, T + a * EXP:T + (a + 1) * EXP], HS[:, a * P:(a + 1) * P], Rw2, start=True, stop=True)
                    last.then_inc(logits_done, 1)
                delta(0)
                turn_x2(0)
                dense(1)
                delta(1)
                turn_x2(1)

            run_slots(pe, slot, step=step)
            run_steps(pe, step, 3)

        @block.scalar
        def _(act):
            def copy(dst, src, **kw):
                return nc.scalar.activation(dst, src, ACT.Copy, **kw)

            def evacuate(hf, it, n, unit, rope, bias, kind=None):
                u, place, _ = unit(hf, it, n)
                q = proj_ps[place][:, 0:T]
                act.wait_ge(projected, u + 1)
                if kind is not None:
                    tile, par = kind
                    nb = it * 2 + (hf * BATCH + n // HEADS + 1)
                    above(act, mixed_v, nb * HEADS - HEADS)
                    copy(V[0][:, par, tile, :], q).then_inc(evacuated, 1)
                    return
                if isinstance(u, int) and u == 0:
                    act.wait_ge(const_in, 16 * len(CONSTS))
                r, rp, _ = rope(hf, it, n)
                above(act, rotated, r - 1)
                nc.scalar.activation(QB[:, rp, :], q, ACT.Identity, bias=bias).then_inc(evacuated, 1)

            def slot(hf, it, n):
                m = n % HEADS
                if live(hf, it, n, L_PT):
                    g, i = head(hf, it, n, L_PT), (n - L_PT) % 2
                    act.wait_ge(turned, g + 1)
                    above(act, mixed_v, g - 1)
                    copy(PT[0][:, i, :], pt_ps[:, 0:P + T]).then_inc(pt_hi, 1)
                if m == 1 and more(hf, it, n):
                    nb = it * 2 + (hf * BATCH + n // HEADS + 1)
                    act.wait_ge(x_in, 16 * nb + 16)
                    if not isinstance(nb, int) or nb >= 2:
                        act.wait_ge(projected, unit_q(hf, it, n // HEADS * HEADS - 1)[0] + 1)
                    copy(X[0][:, (n // HEADS + 1) % 2, :, :], XR[:, :, :]).then_inc(x_hi, 1)
                for r, rp, _, dst, used in rotations(hf, it, n):
                    act.wait_ge(summed, r + 1)
                    above(act, scored, used)
                    copy(dst[0], RF[:, rp, :]).then_inc(rope_hi, 1)
                if live(hf, it, n, L_S):
                    g, i = head(hf, it, n, L_S), (n - L_S) % 2
                    act.wait_ge(maxed, g + 1)
                    for t, c in ((0, slice(0, P)), (1, slice(P, P + T))):
                        last = nc.scalar.activation(S[:, i, c], S[:, i, c], ACT.Exp, bias=NM[:, i, t:t + 1],
                                                    scale=-1.0, accum_out=L[:, i, t:t + 1])
                    last.then_inc(exped, 1)
                if live(hf, it, n, 0):
                    evacuate(hf, it, n, unit_q, rope_q, Bq[:, hf, m:m + 1])
                if live(hf, it, n, L_PV):
                    g, i = head(hf, it, n, L_PV), (n - L_PV) % SLOTS
                    act.wait_ge(mixed_v, g + 1)
                    above(act, wo_done, g - 1)
                    j, p = (i % HEADS) // GROUP, pass_of(hf, it, n, L_PV)
                    nc.scalar.activation(OT[0][:, i % 2, :], ot_ps[:, 0:T], ACT.Identity,
                                         bias=Bv[:, p, j:j + 1]).then_inc(ot_hi, 1)
                e = extra(hf, it, n)
                if e:
                    kind, tile, par = e
                    if kind == "V":
                        evacuate(hf, it, n, unit_x, None, None, (tile, par))
                    else:
                        evacuate(hf, it, n, unit_x, rope_x, Bk[:, next_batch(hf, it, n)[0], tile:tile + 1])
                if hf == 1:
                    tail(it, n, 0)
                if live(hf, it, n, L_S):
                    g, i = head(hf, it, n, L_S), (n - L_S) % 2
                    act.wait_ge(inverted, g + 1)
                    copy(S[:, i, 0:P], S[:, i, 0:P], scale=RL[:, i, 0:1])
                    copy(S[:, i, P:P + T], S[:, i, P:P + T], scale=RL[:, i, 1:2]).then_inc(normed, 1)
                if hf == 1:
                    tail(it, n, 1)

            def tail(it, n, part):
                def at(lag, p):
                    return part == p and tail_live(it, n, lag)

                for t in range(TT):
                    if at((3 if t == 0 else 3), 1):
                        b = batch(0, it, n, L_TAIL + (3 if t == 0 else 3))
                        act.wait_ge(x1_turned, TT * b + t + 1)
                        above(act, d_done, b)
                        above(act, e2_arg, b)
                        if isinstance(it, int) and b == 0:
                            act.wait_ge(w_lo, HALVES * NP)
                        copy(KT[:, :, t * P:(t + 1) * P], tail_ps[:, :].rearrange("p (c t) -> p c t", c=KC)).then_inc(kt_copied, 1)
                if at(5, 1):
                    b = batch(0, it, n, L_TAIL + 5)
                    act.wait_ge(a2_arg, b + 1)
                    nc.scalar.activation(A2[:, :, :], A2[:, :, :], ACT.Exp).then_inc(a2_done, 1)
                if at(6, 0):
                    b = batch(0, it, n, L_TAIL + 6)
                    act.wait_ge(e2_arg, b + 1)
                    nc.scalar.activation(E2[:, :, :], E2[:, :, :], ACT.Exp).then_inc(e2_done, 1)
                if at(6, 1):
                    b = batch(0, it, n, L_TAIL + 6)
                    act.wait_ge(ad_arg, b + 1)
                    nc.scalar.activation(AD[:, :, :], AD[:, :, :], ACT.Exp).then_inc(ad_done, 1)
                if at(7, 0):
                    b = batch(0, it, n, L_TAIL + 7)
                    act.wait_ge(ed_arg, b + 1)
                    nc.scalar.activation(ED[:, :, :], ED[:, :, :], ACT.Exp).then_inc(ed_done, 1)

            def step(it, n):
                def x_hi_tile(lag, t):
                    if stage_live(it, n, lag):
                        b, par = it * 2 + (n - lag), (n - lag) % 2
                        above(act, f_mm, TT * (b - 2) + (t + 1))
                        act.wait_ge(f_turned, TT * b + (t + 1))
                        if isinstance(it, int) and b == 0 and t == 0:
                            act.wait_ge(projected, unit_q(1, TURNS - 1, SLOTS - 1)[0] + 1)
                        copy(X[0][:, par, :, t * P:(t + 1) * P], bank[t][:, :].rearrange("p (c t) -> p c t", c=KC)).then_inc(xt_hi, 1)

                x_hi_tile(2, 1)
                if stage_live(it, n, 2):
                    b = it * 2 + (n - 2)
                    act.wait_ge(hid_done, b + 1)
                    above(act, hid_1p, b)
                    nc.scalar.activation(HE, bank[2][0:HID, 0:T], ACT.Exp, bias=NRb1, scale=-1.0).then_inc(hid_exp, 1)
                if stage_live(it, n, 3):
                    b = it * 2 + (n - 3)
                    act.wait_ge(wt_turned, b + 1)
                    above(act, f_mm, TT * b)
                    copy(WT[0][:, :, :], bank[7][:, :].rearrange("p (r t) -> p r t", r=ER)).then_inc(wt_hi, 1)
                if stage_live(it, n, 2):
                    b = it * 2 + (n - 2)
                    act.wait_ge(top_diff, b + 1)
                    nc.scalar.activation(EM, DM, ACT.Exp).then_inc(top_exp, 1)
                x_hi_tile(1, 0)

            def weights(hf, i):
                u = hf * NP + i
                act.wait_ge(stage_in[u % 4], 16 * (u // 4 + 1))
                if hf == 1:
                    if i < JL + TT:
                        act.wait_ge(projected, unit_x(0, TURNS - 1, HEADS - 1)[0] + 1)
                    elif i < JL + TT + HEADS:
                        act.wait_ge(projected, unit_q(0, TURNS - 1, HEADS + i - JL - TT)[0] + 1)
                    else:
                        act.wait_ge(wo_done, ALL - HEADS + i - JL - TT - HEADS + 1)
                copy(PIECES[hf][i][0][0], stage[:, u % 4, :]).then_inc(w_hi, 1)

            def ffn_weights(i):
                if i == 0:
                    act.wait_ge(projected, unit_q(1, TURNS - 1, SLOTS - 1)[0] + 1)
                act.wait_ge(f_stage_in[i % 2], 16 * (i // 2 + 1))
                copy(FFN[i][0][0], ffn_stage(i)).then_inc(w_hi, 1)

            run_slots(act, slot, weights, ffn_weights, step)
            run_steps(act, step, 3)

        @block.gpsimd
        def _(pool):
            gp = nc.gpsimd

            def rotate(r, rp, nth):
                pool.wait_ge(swapped[rp], nth * 32)
                above(pool, summed, r - 1)
                gp.tensor_tensor(RC[:, rp, :], QB[:, rp, :], Cos[:, :], ALU.mult)
                gp.tensor_tensor(RSN[:, rp, :], SW[:, rp, :], Sin[:, :], ALU.mult).then_inc(rotated, 1)

            def slot(hf, it, n):
                if live(hf, it, n, L_ROPE):
                    rotate(*rope_q(hf, it, n - L_ROPE))
                e = extra(hf, it, n - L_ROPE)
                if e and e[0] == "K":
                    rotate(*rope_x(hf, it, n - L_ROPE))
                if live(hf, it, n, 8, HEADS) and pass_of(hf, it, n, 8) == 0:
                    b, par = batch(hf, it, n, 8), ((n - 8) // HEADS) % 2
                    pool.wait_ge(n_in[par], pair(hf, it, n, 8) * 16)
                    gp.tensor_tensor(XN[:, par, 0, :], XN[:, par, 0, :], Bo[:, :], ALU.add)
                    gp.tensor_tensor(XN[:, par, 1, :], XN[:, par, 1, :], Bo[:, :], ALU.add).then_inc(n_sum, 1)
                if hf == 1:
                    tail(it, n)

            def tail(it, n):
                def at(lag):
                    return tail_live(it, n, lag)

                def bp(lag):
                    return batch(0, it, n, L_TAIL + lag), ((n - L_TAIL - lag) // HEADS) % 2
                if at(0):
                    b, par = bp(0)
                    pool.wait_ge(x1_ve, b + 1)
                    gp.tensor_tensor(RS[:, par, :], VE[:, par, :], Mhalf[:, :], ALU.pow).then_inc(x1_rs, 1)
                if at(5):
                    b, _ = bp(5)
                    pool.wait_ge(mx_done, b + 1)
                    above(pool, qs_done, b)
                    gp.tensor_tensor(E2[:, :, :], KT[:, :, :], MX[:, :, 1:T + 1], ALU.subtract).then_inc(e2_arg, 1)
                if at(6):
                    b, _ = bp(6)
                    pool.wait_ge(e2_done, b + 1)
                    pool.wait_ge(v_in, 16 * b + 16)
                    above(pool, y_turned, TT * b)
                    gp.tensor_tensor(EV[:, :, :], E2[:, :, :], VT[:, :, :], ALU.mult).then_inc(e2v_done, 1)
                if at(7):
                    b, _ = bp(7)
                    pool.wait_ge(qs_done, b + 1)
                    pool.wait_ge(ad_done, b + 1)
                    gp.tensor_tensor(QS[:, :, 0:T], QS[:, :, 0:T], AD[:, :, :], ALU.mult).then_inc(aq_done, 1)
                if at(8):
                    b, _ = bp(8)
                    pool.wait_ge(ed_done, b + 1)
                    pool.wait_ge(ps_done, b + 1)
                    gp.tensor_tensor(EV[:, :, :], ED[:, :, :], VT[:, :, :], ALU.mult).then_inc(ev_done, 1)
                    pool.wait_ge(aq_done, b + 1)
                    gp.tensor_tensor(AD[:, :, :], PS[:, :, 0:T], AD[:, :, :], ALU.mult).then_inc(ap_done, 1)
                if at(9):
                    b, _ = bp(9)
                    pool.wait_ge(ap_done, b + 1)
                    gp.tensor_tensor(EV[:, :, :], EV[:, :, :], AD[:, :, :], ALU.add).then_inc(num_done, 1)
                if at(10):
                    b, _ = bp(10)
                    pool.wait_ge(num_done, b + 1)
                    pool.wait_ge(den_done, b + 1)
                    gp.tensor_tensor(EV[:, 0::2, :], EV[:, 0::2, :], A2[:, 1::2, :], ALU.mult)
                    gp.tensor_tensor(EV[:, 1::2, :], EV[:, 1::2, :], A2[:, 0::2, :], ALU.mult).then_inc(cross_done, 1)
                if at(L_Y + 2):
                    b, par = bp(L_Y + 2)
                    pool.wait_ge(x2_ve, b + 1)
                    gp.tensor_tensor(RS2[:, par, :], VE2[:, par, :], Mhalf[:, :], ALU.pow).then_inc(x2_rs, 1)

            def step(it, n):
                if stage_live(it, n, 2):
                    b, par = it * 2 + (n - 2), (n - 2) % 2
                    pool.wait_ge(f_turned, TT * b + TT)
                    above(pool, f_sum, TT * (b - 1))
                    if isinstance(it, int) and b == 0:
                        pool.wait_ge(fb_in, 16)
                        pool.wait_ge(turned, HALVES * ALL)
                    for t in range(TT):
                        last = gp.tensor_tensor(X2B[par][t], XN[:, par, t, :], Fb[:, :], ALU.add)
                    last.then_inc(biased, 1)
                if stage_live(it, n, 4):
                    b, par = it * 2 + (n - 4), (n - 4) % 2
                    pool.wait_ge(f_ve, b + 1)
                    gp.tensor_tensor(RS[:, par, :], VE[:, par, :], Mhalf[:, :], ALU.pow).then_inc(f_rs, 1)

            pool.wait_ge(const_in, 16 * len(CONSTS))
            gp.tensor_scalar(NRb1, Rb1, -1.0, None, ALU.mult)
            gp.memset(Mhalf[:, :], -0.5)
            gp.memset(MX[:, :, 0:1], NEG)
            gp.memset(PS[:, :, 0:1], 0.0)
            gp.memset(QS[:, :, 0:1], 0.0).then_inc(consts, 1)
            pool.wait_ge(consts, 1)
            run_slots(pool, slot, step=step)
            run_steps(pool, step, 4)

        @block.vector
        def _(dve):
            v = nc.vector

            def slot(hf, it, n):
                m = n % HEADS
                us = rotations(hf, it, n)
                for r, rp, _, dst, used in us:
                    dve.wait_ge(rotated, r + 1)
                    above(dve, rope_lo, r - 1)
                    v.tensor_tensor(RF[:, rp, :], RC[:, rp, :], RSN[:, rp, :], ALU.add).then_inc(summed, 1)
                s_live = live(hf, it, n, L_S)
                if s_live:
                    g, i = head(hf, it, n, L_S), (n - L_S) % 2
                    if isinstance(g, int) and g == 0:
                        dve.wait_ge(const_in, 16 * len(CONSTS))
                        dve.wait_ge(consts, 1)
                    dve.wait_ge(scored, g + 1)
                    above(dve, turned, g - 1)
                if live(hf, it, n, L_OTL):
                    g, i = head(hf, it, n, L_OTL), (n - L_OTL) % SLOTS
                    j = (i % HEADS) // GROUP
                    dve.wait_ge(ot_hi, g + 1)
                    v.scalar_tensor_tensor(out=OT[1][:, i % 2, :], in0=ot_ps[:, 0:T],
                                           scalar=Bv[:, pass_of(hf, it, n, L_OTL), j:j + 1],
                                           in1=OT[0][:, i % 2, :], op0=ALU.add, op1=ALU.subtract).then_inc(ot_lo, 1)
                if s_live:
                    g, i = head(hf, it, n, L_S), (n - L_S) % 2
                    for t, c in ((0, slice(0, P)), (1, slice(P, P + T))):
                        last = v.tensor_tensor_reduce(out=S[:, i, c], in0=s_ps[:, c], in1=Mask[:, c], scale=-SCALE,
                                                      scalar=3e38, op0=ALU.add, op1=ALU.min, accum_out=NM[:, i, t:t + 1])
                    last.then_inc(maxed, 1)
                if live(hf, it, n, L_TAIL, HEADS):
                    b, par = batch(hf, it, n, L_TAIL), ((n - L_TAIL) // HEADS) % 2
                    dve.wait_ge(wo_done, HEADS * b + HEADS)
                    dve.wait_ge(n_in[par], pair(hf, it, n, L_TAIL) * 16)
                    p = pass_of(hf, it, n, L_TAIL)
                    if p == 0:
                        dve.wait_ge(n_sum, b + 1)
                    if p == 1 and isinstance(b, int) and b < BATCH + 2:
                        dve.wait_ge(r_out[par], 16 * BATCH // 2)
                    else:
                        above(dve, (r_out, x2_out)[p][par], (pair(hf - p, it, n, L_TAIL) - 1) * 16)
                    for t in range(TT):
                        last = v.tensor_tensor(RO[:, par, t, :], acc_ps[t][:, :], XN[:, par, t, :], ALU.add)
                    last.then_inc(acc_read, 1)
                for r, rp, _, dst, used in us:
                    dve.wait_ge(rope_hi, r + 1)
                    v.tensor_tensor(dst[1], RF[:, rp, :], dst[0], ALU.subtract).then_inc(rope_lo, 1)
                if hf == 1:
                    tail(it, n, 0)
                if live(hf, it, n, L_PT):
                    g, i = head(hf, it, n, L_PT), (n - L_PT) % 2
                    dve.wait_ge(pt_hi, g + 1)
                    v.tensor_tensor(PT[1][:, i, :], pt_ps[:, 0:P + T], PT[0][:, i, :], ALU.subtract).then_inc(pt_lo, 1)
                if m == X_LO and more(hf, it, n):
                    nb = it * 2 + (hf * BATCH + n // HEADS + 1)
                    dve.wait_ge(x_hi, nb + 1)
                    par = (n // HEADS + 1) % 2
                    v.tensor_tensor(X[1][:, par, :, :], XR[:, :, :], X[0][:, par, :, :], ALU.subtract).then_inc(x_lo, 1)
                if s_live:
                    g, i = head(hf, it, n, L_S), (n - L_S) % 2
                    dve.wait_ge(exped, g + 1)
                    v.reciprocal(RL[:, i, :], L[:, i, :]).then_inc(inverted, 1)
                e = extra(hf, it, n)
                if e and e[0] == "V":
                    u, place, _ = unit_x(hf, it, n)
                    dve.wait_ge(evacuated, u + 1)
                    v.tensor_tensor(V[1][:, e[2], e[1], :], proj_ps[place][:, 0:T], V[0][:, e[2], e[1], :],
                                    ALU.subtract).then_inc(v_lo, 1)
                if hf == 1:
                    tail(it, n, 1)
                if hf == 1:
                    tail(it, n, 2)

            def norm_stats(tiles, par, ready, value, stats, mv, ve, done):
                dve.wait_ge(ready, value)
                for t in range(TT):
                    v.bn_stats(stats[:, par, t, :], tiles[:, t, :])
                dve.drain()
                for t in range(TT):
                    v.bn_aggr(mv[:, par, t, :], stats[:, par, t, :])
                dve.drain()
                v.tensor_scalar(ve[:, par, :], mv[:, par, :, 1], EPS, None, ALU.add).then_inc(done, 1)

            def norm_apply(tiles, par, mv, rs, done):
                for t in range(TT):
                    last = v.tensor_scalar(tiles[:, t, :], tiles[:, t, :], mv[:, par, t, 0:1], rs[:, par, t:t + 1],
                                           ALU.subtract, ALU.mult)
                last.then_inc(done, 1)

            def tail(it, n, part):
                def at(lag, p):
                    return part == p and tail_live(it, n, lag)

                def bp(lag):
                    return batch(0, it, n, L_TAIL + lag), ((n - L_TAIL - lag) // HEADS) % 2
                if at(0, 2):
                    b, par = bp(0)
                    norm_stats(RO[:, par, :, :], par, acc_read, BATCH + b + 1, ST, MV, VE, x1_ve)
                if at(1, 1):
                    b, par = bp(1)
                    dve.wait_ge(x1_rs, b + 1)
                    norm_apply(RO[:, par, :, :], par, MV, RS, x1_done)
                if at(4, 1):
                    b, _ = bp(4)
                    dve.wait_ge(kt_copied, TT * b + TT)
                    above(dve, e2_arg, b)
                    for c in range(KC):
                        last = v.tensor_tensor_scan(MX[:, c, 1:T + 1], Wb[:, c:c + 1].to_broadcast([P, T]), KT[:, c, :], NEG, ALU.add, ALU.max)
                    last.then_inc(mx_done, 1)
                if at(4, 2):
                    b, _ = bp(4)
                    dve.wait_ge(mx_done, b + 1)
                    for c in range(KC):
                        last = v.scalar_tensor_tensor(out=A2[:, c, :], in0=MX[:, c, 0:T], scalar=Wb[:, c:c + 1],
                                                      in1=MX[:, c, 1:T + 1], op0=ALU.add, op1=ALU.subtract)
                    last.then_inc(a2_arg, 1)
                if at(5, 0):
                    b, _ = bp(5)
                    for c in range(KC):
                        last = v.scalar_tensor_tensor(out=AD[:, c, :], in0=KT[:, c, :], scalar=Ub[:, c:c + 1],
                                                      in1=MX[:, c, 0:T], op0=ALU.add, op1=ALU.subtract)
                    last.then_inc(d_done, 1)
                if at(5, 1):
                    b, _ = bp(5)
                    dve.wait_ge(d_done, b + 1)
                    v.tensor_scalar(ED[:, :, :], AD[:, :, :], 0.0, None, ALU.min).then_inc(ed_arg, 1)
                if at(5, 2):
                    b, _ = bp(5)
                    v.tensor_scalar(AD[:, :, :], AD[:, :, :], 0.0, -1.0, ALU.max, ALU.mult).then_inc(ad_arg, 1)
                if at(6, 1):
                    b, _ = bp(6)
                    dve.wait_ge(a2_done, b + 1)
                    dve.wait_ge(e2_done, b + 1)
                    for c in range(KC):
                        last = v.tensor_tensor_scan(QS[:, c, 1:T + 1], A2[:, c, :], E2[:, c, :], 0.0, ALU.mult, ALU.add)
                    last.then_inc(qs_done, 1)
                if at(7, 0):
                    b, _ = bp(7)
                    dve.wait_ge(e2v_done, b + 1)
                    for c in range(KC):
                        last = v.tensor_tensor_scan(PS[:, c, 1:T + 1], A2[:, c, :], EV[:, c, :], 0.0, ALU.mult, ALU.add)
                    last.then_inc(ps_done, 1)
                if at(9, 0):
                    b, _ = bp(9)
                    dve.wait_ge(aq_done, b + 1)
                    dve.wait_ge(ed_done, b + 1)
                    dve.wait_ge(ps_done, b + 1)
                    v.tensor_tensor(A2[:, :, :], QS[:, :, 0:T], ED[:, :, :], ALU.add).then_inc(den_done, 1)
                if at(9, 1):
                    b, _ = bp(9)
                    dve.wait_ge(den_done, b + 1)
                    dve.wait_ge(ev_done, b + 1)
                    v.tensor_tensor(ED[:, 0:2, :], A2[:, 0::2, :], A2[:, 1::2, :], ALU.mult).then_inc(pairs_done, 1)
                if at(9, 2):
                    b, _ = bp(9)
                    dve.wait_ge(pairs_done, b + 1)
                    v.tensor_tensor(ED[:, 2, :], ED[:, 0, :], ED[:, 1, :], ALU.mult).then_inc(quad_done, 1)
                if at(10, 0):
                    b, _ = bp(10)
                    dve.wait_ge(quad_done, b + 1)
                    v.reciprocal(ED[:, 3, :], ED[:, 2, :]).then_inc(rquad_done, 1)
                if at(10, 2):
                    b, _ = bp(10)
                    dve.wait_ge(rquad_done, b + 1)
                    dve.wait_ge(num_done, b + 1)
                    v.tensor_tensor(AD[:, 0, :], ED[:, 3, :], ED[:, 1, :], ALU.mult)
                    v.tensor_tensor(AD[:, 1, :], ED[:, 3, :], ED[:, 0, :], ALU.mult).then_inc(rden_done, 1)
                if at(11, 2):
                    b, _ = bp(11)
                    dve.wait_ge(rden_done, b + 1)
                    dve.wait_ge(cross_done, b + 1)
                    for c in range(0, KC, 2):
                        last = v.tensor_tensor(EV[:, c:c + 2, :], EV[:, c:c + 2, :],
                                               AD[:, c // 2:c // 2 + 1, :].to_broadcast([P, 2, T]), ALU.mult)
                    last.then_inc(y_done, 1)
                for t in range(TT):
                    if at(L_Y + 1 + t, 0):
                        b, par = bp(L_Y + 1 + t)
                        dve.wait_ge(y_turned, TT * b + t + 1)
                        v.tensor_tensor(RO[:, par, t, :], tail_ps[:, :], RO[:, par, t, :], ALU.add).then_inc(x2_sum, 1)
                if at(L_Y + 2, 1):
                    b, par = bp(L_Y + 2)
                    norm_stats(RO[:, par, :, :], par, x2_sum, TT * b + TT, ST2, MV2, VE2, x2_ve)
                if at(L_Y + 3, 0):
                    b, par = bp(L_Y + 3)
                    dve.wait_ge(x2_rs, b + 1)
                    norm_apply(RO[:, par, :, :], par, MV2, RS2, x2_done)

            def step(it, n):
                def x_lo_tile(lag, t):
                    if stage_live(it, n, lag):
                        b, par = it * 2 + (n - lag), (n - lag) % 2
                        dve.wait_ge(xt_hi, TT * b + (t + 1))
                        v.tensor_tensor(X[1][:, par, :, t * P:(t + 1) * P], bank[t][:, :].rearrange("p (c t) -> p c t", c=KC),
                                        X[0][:, par, :, t * P:(t + 1) * P], ALU.subtract).then_inc(xt_lo, 1)

                def out_sum(lag, t):
                    if stage_live(it, n, lag):
                        b, par = it * 2 + (n - lag), (n - lag) % 2
                        dve.wait_ge(f_mm, TT * b + (t + 1))
                        if t == 0:
                            dve.wait_ge(biased, b + 1)
                            above(dve, f_out[par], (it + ((n - lag) // 2)) * 16)
                            if isinstance(it, int) and b == 0:
                                dve.wait_ge(x2_out[0], 16 * BATCH // 2)
                        v.tensor_tensor(OUT[par][:, t, :], bank[5 + t][:, :], X2B[par][t], ALU.add).then_inc(f_sum, 1)

                x_lo_tile(2, 1)
                out_sum(4, 1)
                if stage_live(it, n, 4):
                    norm_stats(OUT[n % 2], n % 2, f_sum, it * (2 * TT) + TT * (n - 3), ST, MV, VE, f_ve)
                if stage_live(it, n, 2):
                    b = it * 2 + (n - 2)
                    dve.wait_ge(hid_exp, b + 1)
                    above(dve, logits_done, b)
                    v.tensor_scalar(HS, HE, 1.0, None, ALU.add).then_inc(hid_1p, 1)
                    dve.wait_ge(hid_1p, b + 1)
                    v.reciprocal(HS, HS).then_inc(hid_inv, 1)
                    dve.wait_ge(hid_inv, b + 1)
                    v.scalar_tensor_tensor(out=HS, in0=bank[2][0:HID, 0:T], scalar=Rb1, in1=HS, op0=ALU.add, op1=ALU.mult).then_inc(silu_done, 1)
                if stage_live(it, n, 3):
                    b = it * 2 + (n - 3)
                    dve.wait_ge(wt_hi, b + 1)
                    v.tensor_tensor(WT[1][:, :, :], bank[7][:, :].rearrange("p (r t) -> p r t", r=ER), WT[0][:, :, :], ALU.subtract).then_inc(wt_lo, 1)
                if stage_live(it, n, 4):
                    b = it * 2 + (n - 4)
                    dve.wait_ge(f_rs, b + 1)
                    norm_apply(OUT[n % 2], n % 2, MV, RS, f_done)
                if stage_live(it, n, 2):
                    b = it * 2 + (n - 2)
                    dve.wait_ge(logits_done, b + 1)
                    lgp = bank[2][:, T:T + TT * EXP].rearrange("p (a e) -> p a e", e=EXP)
                    for t in range(TT):
                        last = v.tensor_tensor(LG0[:, t, :], lgp[:, t, :], Rb2, ALU.add)
                    last.then_inc(lg_b, 1)
                    dve.wait_ge(lg_b, b + 1)
                    for t in range(TT):
                        last = v.tensor_tensor(LG[:, t, :], LG0[:, t, :], Gates, ALU.add)
                    last.then_inc(lg_g, 1)
                    dve.drain()
                    for t in range(TT):
                        v.max(M8[:, t, :], LG[:, t, :])
                    dve.drain()
                    v.tensor_tensor(DM, M8[:, :, 1:2], M8[:, :, 0:1], ALU.subtract).then_inc(top_diff, 1)
                    for t in range(TT):
                        v.max_index(IX[:, t, :], M8[:, t, :], LG[:, t, :])
                    dve.drain()
                    v.tensor_copy(I8, IX).then_inc(lg_sum, 1)
                out_sum(3, 0)
                x_lo_tile(1, 0)
                if stage_live(it, n, 2):
                    b = it * 2 + (n - 2)
                    dve.wait_ge(top_exp, b + 1)
                    v.tensor_scalar(SE, EM, 1.0, None, ALU.add).then_inc(top_sum, 1)
                    dve.wait_ge(top_sum, b + 1)
                    v.reciprocal(P1, SE).then_inc(top_p1, 1)
                    dve.wait_ge(top_p1, b + 1)
                    v.tensor_tensor(P2, EM, P1, ALU.mult).then_inc(top_p2, 1)
                    dve.wait_ge(top_p2, b + 1)
                    dve.wait_ge(lg_sum, b + 1)
                    for t in range(TT):
                        v.tensor_scalar(C1[:, t, :], Iota, I8[:, t, 0:1], P1[:, t, :], ALU.is_equal, ALU.mult)
                        last = v.tensor_scalar(C2[:, t, :], Iota, I8[:, t, 1:2], P2[:, t, :], ALU.is_equal, ALU.mult)
                    last.then_inc(coef_parts, 1)
                    dve.wait_ge(coef_parts, b + 1)
                    v.tensor_tensor(CF, C1, C2, ALU.add).then_inc(coef_done, 1)
                    dve.wait_ge(coef_done, b + 1)
                    dve.wait_ge(low_done, TT * b + TT)
                    above(dve, wt_turned, b)
                    for t in range(TT):
                        last = v.tensor_tensor(WX[:, t, :].rearrange("p (e r) -> p e r", e=EXP),
                                               bank[3 + n % 2][:, t * T:(t + 1) * T].rearrange("p (e r) -> p e r", e=EXP),
                                               CF[:, t, :].rearrange("p (e r) -> p e r", r=1).to_broadcast([P, EXP, RANK]), ALU.mult)
                    last.then_inc(weighted, 1)

            def weights(hf, i):
                u = hf * NP + i
                dve.wait_ge(w_hi, u + 1)
                (hi, lo), _ = PIECES[hf][i]
                v.tensor_tensor(lo, stage[:, u % 4, :], hi, ALU.subtract).then_inc(w_lo, 1)

            def ffn_weights(i):
                dve.wait_ge(w_hi, HALVES * NP + i + 1)
                (hi, lo), _ = FFN[i]
                v.tensor_tensor(lo, ffn_stage(i), hi, ALU.subtract).then_inc(w_lo, 1)

            run_slots(dve, slot, weights, ffn_weights, step)
            run_steps(dve, step, 4)


def layouts(i):
    g = lambda n: np.asarray(i[n])
    x, ctx = g("x"), g("ctx_2048")
    order = np.concatenate([np.arange(0, HD, 2), np.arange(1, HD, 2)])
    heads = np.array([[g_ * HKV + hf * JL + jl for jl in range(JL) for g_ in range(GROUP)] for hf in range(HALVES)])
    wq = g("L0_attn_Wq").reshape(KC, P, H, HD)[:, :, heads][..., order]
    wk = g("L0_attn_Wk").reshape(KC, P, HALVES, JL, HD)[..., order]
    wv = g("L0_attn_Wv").reshape(KC, P, HALVES, JL * HD)
    wo = g("L0_attn_Wo").reshape(H, HD, C)[heads]
    e = EXP
    row = lambda a: np.broadcast_to(a, (P, a.shape[0]))
    return dict(
        xt=x.reshape(BATCH, T, KC, P).transpose(0, 3, 2, 1), xn=x,
        ctxt=ctx.reshape(BATCH, T, KC, P).transpose(0, 3, 2, 1),
        wq=wq.transpose(2, 1, 3, 0, 4), wk=wk.transpose(2, 1, 3, 0, 4), wv=wv.transpose(2, 1, 0, 3),
        wo=wo.transpose(0, 2, 1, 3),
        bq=g("L0_attn_bq").reshape(H, HD)[heads][..., order].transpose(2, 0, 1),
        bk=g("L0_attn_bk").reshape(HALVES, JL, HD)[..., order].transpose(2, 0, 1),
        bv=g("L0_attn_bv").reshape(HALVES, JL, HD).transpose(2, 0, 1),
        bo=row(g("L0_attn_bo")),
        wdec=g("L0_xattn_w").reshape(KC, P).T, ubon=g("L0_xattn_u").reshape(KC, P).T,
        wf=g("L0_ffn_W").T.reshape(KC, P, C).transpose(1, 0, 2),
        wa=g("L0_ffn_A").reshape(EXP * RANK, KC, P).transpose(2, 1, 0),
        wb=g("L0_ffn_B").transpose(0, 2, 1).reshape(ER, P, C).transpose(1, 0, 2),
        rw1=np.concatenate([g("L0_ffn_rw1"), np.zeros((P - HID, C), x.dtype)]).reshape(P, KC, P).transpose(2, 1, 0),
        rw2=g("L0_ffn_rw2")[:e].T, fbias=row(g("L0_ffn_bias")), rb1=g("L0_ffn_rb1").reshape(HID, 1),
        rb2=row(g("L0_ffn_rb2")[:e]), gates=row(g("L0_ffn_gates")),
    )


def tables():
    theta = np.float32(1.0) / np.float32(10000.0) ** (np.arange(0, HD, 2, dtype=np.float32) / np.float32(HD))
    angle = (np.arange(T, dtype=np.float32)[None, :] * theta[:, None]).astype(np.float32)
    c, s = (f(angle.astype(np.float64)).astype(np.float32) for f in (np.cos, np.sin))
    tri = np.where(np.arange(P)[None, :] <= np.arange(P)[:, None], 0.0, MASKED).astype(np.float32)
    return dict(cos_t=np.concatenate([c, c]), sin_t=np.concatenate([-s, s]),
                mask_t=np.concatenate([tri, np.zeros((P, P), np.float32), tri], axis=1),
                ident_t=np.eye(P, dtype=np.float32),
                iota_t=np.broadcast_to(np.arange(EXP, dtype=np.float32), (P, EXP)))


def kernel(**inputs):
    import concourse.bacc as bacc
    from concourse.bass_utils import run_bass_kernel_spmd as run

    nc = bacc.Bacc("TRN2", target_bir_lowering=False, num_devices=1)
    arrays, args = {}, {}
    for name, a in (layouts(inputs) | tables()).items():
        arrays[f"in_{name}"] = a = np.ascontiguousarray(a)
        args[name] = nc.dram_tensor(f"in_{name}", a.shape, mybir.dt.from_np(a.dtype), kind="ExternalInput").ap()
    args["out"] = nc.dram_tensor("out_x", (BATCH, T, C), mybir.dt.float32, kind="ExternalOutput").ap()
    decoder(nc, **args)
    return run(nc, [arrays], core_ids=[0]).results[0]["out_x"]
```
